# Optimizing a Trainium2 kernel written in Bass

```python
import numpy as np
import jax
import jax.numpy as jnp

def _softmax(x, axis=-1):
    return jax.nn.softmax(x, axis=axis)

def _gelu(x):
    return jax.nn.gelu(x, approximate=True)

def _silu(x):
    return jax.nn.silu(x)

def _sigmoid(x):
    return jax.nn.sigmoid(x)

def _layernorm(x, axis=-1, eps=1e-05):
    m = jnp.mean(x, axis=axis, keepdims=True)
    v = jnp.var(x, axis=axis, keepdims=True)
    return (x - m) / jnp.sqrt(v + eps)

def _scatter_add(tgt, idx, src, axis=0):
    return tgt.at[idx].add(src)

def _segment_sum(src, seg, n):
    return jax.ops.segment_sum(src, seg, n)
kernel_name = 'mk_audio_tower_d1_tok_audfeat768_r4_1bbe32'

def setup_inputs(seed: int=0):
    np.random.seed(seed)
    _w = jnp.asarray

    def _rec_inputs():
        import jax
        import jax.numpy as jnp
        _rk = jax.random.key(seed)
        x = -0.000183583 + 0.999963 * jax.random.normal(jax.random.fold_in(_rk, 1), (8, 750, 192), jnp.float32)
        return x
    x = _rec_inputs()

    def _L0_tok_setup():
        import jax, jax.numpy as jnp
        import numpy as np
        KEEP_RATIO = 0.7
        key = jax.random.key(seed)
        kx, kw = jax.random.split(key)
        B, N, D = (32, 1024, 192)
        x = jax.random.normal(kx, (B, N, D), dtype=jnp.float32)
        w = jax.random.normal(kw, (D, 1), dtype=jnp.float32) * (1.0 / np.sqrt(D))
        b = jnp.zeros((1,), dtype=jnp.float32)
        return {'x': x, 'w': w, 'b': b}
    _L0_tok_all = _L0_tok_setup()
    _L0_tok_in = {k: v for k, v in _L0_tok_all.items() if k in ('w', 'b')}
    del _L0_tok_all

    def _L0_attn_setup():
        import jax, jax.numpy as jnp
        import numpy as np
        DIM = 192
        HEADS = 12
        DH = DIM // HEADS
        M = 64
        EPS = 0.0001

        def softmax_kernel(data, proj, is_query):
            data_normalizer = data.shape[-1] ** (-0.25)
            ratio = proj.shape[0] ** (-0.5)
            data_dash = jnp.einsum('bhsd,md->bhsm', data_normalizer * data, proj)
            diag = 0.5 * data_normalizer ** 2 * jnp.sum(data * data, axis=-1, keepdims=True)
            if is_query:
                stab = jnp.max(data_dash, axis=-1, keepdims=True)
            else:
                stab = jnp.max(data_dash, axis=(-2, -1), keepdims=True)
            stab = jax.lax.stop_gradient(stab)
            return ratio * (jnp.exp(data_dash - diag - stab) + EPS)
        key = jax.random.key(seed)
        kx, kq, kk, kv, ko, kp = jax.random.split(key, 6)
        B, S = (8, 1024)
        w_scale = DIM ** (-0.5)
        return {'x': jax.random.normal(kx, (B, S, DIM), jnp.float32), 'Wq': jax.random.normal(kq, (DIM, DIM), jnp.float32) * w_scale, 'Wk': jax.random.normal(kk, (DIM, DIM), jnp.float32) * w_scale, 'Wv': jax.random.normal(kv, (DIM, DIM), jnp.float32) * w_scale, 'Wo': jax.random.normal(ko, (DIM, DIM), jnp.float32) * w_scale, 'proj': jax.random.normal(kp, (M, DH), jnp.float32)}
    _L0_attn_all = _L0_attn_setup()
    _L0_attn_in = {k: v for k, v in _L0_attn_all.items() if k in ('Wq', 'Wk', 'Wv', 'Wo', 'proj')}
    del _L0_attn_all

    def _L0_ffn_setup():
        import jax, jax.numpy as jnp
        import numpy as np
        DIM = 192
        NUM_EXPERTS = 4
        NUM_HEADS = 12
        HEAD_DIM = DIM // NUM_HEADS
        MLP_HID = 4 * DIM
        FC1_OUT = MLP_HID + 3 * DIM
        FC2_IN = MLP_HID + DIM
        FC2_OUT = 2 * DIM
        CAP_FACTOR = 0.5
        LN_EPS = 1e-06
        key = jax.random.key(seed)
        ks = jax.random.split(key, 4)
        B, N = (8, 256)
        return {'x': jax.random.normal(ks[0], (B, N, DIM), jnp.float32), 'w_router': jax.random.normal(ks[1], (NUM_EXPERTS, DIM), jnp.float32) * 0.02, 'gamma1': jnp.ones((DIM,), jnp.float32), 'beta1': jnp.zeros((DIM,), jnp.float32), 'w1': jax.random.normal(ks[2], (FC1_OUT, DIM), jnp.float32) * 0.02, 'b1': jnp.zeros((FC1_OUT,), jnp.float32), 'w2': jax.random.normal(ks[3], (FC2_OUT, FC2_IN), jnp.float32) * 0.02, 'b2': jnp.zeros((FC2_OUT,), jnp.float32)}
    _L0_ffn_all = _L0_ffn_setup()
    _L0_ffn_in = {k: v for k, v in _L0_ffn_all.items() if k in ('w_router', 'gamma1', 'beta1', 'w1', 'b1', 'w2', 'b2')}
    del _L0_ffn_all
    return {'x': x, 'L0_tok_w': _L0_tok_in['w'], 'L0_tok_b': _L0_tok_in['b'], 'L0_attn_Wq': _L0_attn_in['Wq'], 'L0_attn_Wk': _L0_attn_in['Wk'], 'L0_attn_Wv': _L0_attn_in['Wv'], 'L0_attn_Wo': _L0_attn_in['Wo'], 'L0_attn_proj': _L0_attn_in['proj'], 'L0_ffn_w_router': _L0_ffn_in['w_router'], 'L0_ffn_gamma1': _L0_ffn_in['gamma1'], 'L0_ffn_beta1': _L0_ffn_in['beta1'], 'L0_ffn_w1': _L0_ffn_in['w1'], 'L0_ffn_b1': _L0_ffn_in['b1'], 'L0_ffn_w2': _L0_ffn_in['w2'], 'L0_ffn_b2': _L0_ffn_in['b2']}

def reference(x, L0_tok_w, L0_tok_b, L0_attn_Wq, L0_attn_Wk, L0_attn_Wv, L0_attn_Wo, L0_attn_proj, L0_ffn_w_router, L0_ffn_gamma1, L0_ffn_beta1, L0_ffn_w1, L0_ffn_b1, L0_ffn_w2, L0_ffn_b2):
    import jax
    import jax.numpy as jnp

    def _L0_tok_ref(x, w, b):
        import jax, jax.numpy as jnp
        import numpy as np
        KEEP_RATIO = 0.7
        scores = jnp.einsum('bnd,do->bn', x, w) + b[0]
        N = x.shape[1]
        k = int(round(N * KEEP_RATIO))
        _, idx = jax.lax.top_k(scores, k)
        return jnp.take_along_axis(x, idx[:, :, None], axis=1)

    def _L0_attn_ref(x, Wq, Wk, Wv, Wo, proj):
        import jax, jax.numpy as jnp
        import numpy as np
        DIM = 192
        HEADS = 12
        DH = DIM // HEADS
        M = 64
        EPS = 0.0001

        def softmax_kernel(data, proj, is_query):
            data_normalizer = data.shape[-1] ** (-0.25)
            ratio = proj.shape[0] ** (-0.5)
            data_dash = jnp.einsum('bhsd,md->bhsm', data_normalizer * data, proj)
            diag = 0.5 * data_normalizer ** 2 * jnp.sum(data * data, axis=-1, keepdims=True)
            if is_query:
                stab = jnp.max(data_dash, axis=-1, keepdims=True)
            else:
                stab = jnp.max(data_dash, axis=(-2, -1), keepdims=True)
            stab = jax.lax.stop_gradient(stab)
            return ratio * (jnp.exp(data_dash - diag - stab) + EPS)
        B, S, _ = x.shape

        def split_heads(t):
            return t.reshape(B, S, HEADS, DH).transpose(0, 2, 1, 3)
        q = split_heads(x @ Wq)
        k = split_heads(x @ Wk)
        v = split_heads(x @ Wv)
        qp = softmax_kernel(q, proj, is_query=True)
        kp = softmax_kernel(k, proj, is_query=False)
        k_sum = jnp.sum(kp, axis=2)
        d_inv = 1.0 / jnp.einsum('bhsm,bhm->bhs', qp, k_sum)
        ctx = jnp.einsum('bhsm,bhsd->bhmd', kp, v)
        out = jnp.einsum('bhsm,bhmd,bhs->bhsd', qp, ctx, d_inv)
        out = out.transpose(0, 2, 1, 3).reshape(B, S, DIM)
        return out @ Wo

    def _L0_ffn_ref(x, w_router, gamma1, beta1, w1, b1, w2, b2):
        import jax, jax.numpy as jnp
        import numpy as np
        DIM = 192
        NUM_EXPERTS = 4
        NUM_HEADS = 12
        HEAD_DIM = DIM // NUM_HEADS
        MLP_HID = 4 * DIM
        FC1_OUT = MLP_HID + 3 * DIM
        FC2_IN = MLP_HID + DIM
        FC2_OUT = 2 * DIM
        CAP_FACTOR = 0.5
        LN_EPS = 1e-06
        B, N, C = x.shape
        E = NUM_EXPERTS
        cap = int(CAP_FACTOR * N)
        m = np.array([C // 2 ** (E - 1 - e) for e in range(E)])
        in_mask = (np.arange(C)[None, :] < m[:, None]).astype(np.float32)
        in_mask = jnp.asarray(in_mask)
        out_mask = jnp.concatenate([in_mask, in_mask], axis=-1)
        logits = jnp.einsum('bnc,ec->bne', x, w_router)
        probs = jax.nn.softmax(logits, axis=-1)
        gate, idx = jax.lax.top_k(jnp.swapaxes(probs, 1, 2), cap)
        dispatch = jax.nn.one_hot(idx, N, dtype=x.dtype)
        combine = dispatch * gate[..., None]
        mu = jnp.mean(x, -1, keepdims=True)
        var = jnp.var(x, -1, keepdims=True)
        y = (x - mu) * jax.lax.rsqrt(var + LN_EPS) * gamma1 + beta1
        xg = jnp.einsum('becn,bnd->becd', dispatch, y)
        xg = xg * in_mask[None, :, None, :]
        h = jnp.einsum('becd,fd->becf', xg, w1) + b1
        h = jnp.einsum('becn,becf->bnf', dispatch, h)
        x_mlp, x_qkv = (h[..., :MLP_HID], h[..., MLP_HID:])
        qkv = x_qkv.reshape(B, N, 3, NUM_HEADS, HEAD_DIM).transpose(2, 0, 3, 1, 4)
        q, k, v = (qkv[0], qkv[1], qkv[2])
        scale = HEAD_DIM ** (-0.5)
        attn = jax.nn.softmax(jnp.einsum('bhqd,bhkd->bhqk', q, k) * scale, axis=-1)
        x_attn = jnp.einsum('bhqk,bhkd->bhqd', attn, v)
        x_attn = x_attn.transpose(0, 2, 1, 3).reshape(B, N, C)
        x_mlp = jax.nn.gelu(x_mlp, approximate=False)
        y2 = jnp.concatenate([x_mlp, x_attn], axis=-1)
        yg = jnp.einsum('becn,bnf->becf', dispatch, y2)
        o = jnp.einsum('becf,of->beco', yg, w2) + b2
        o = o * out_mask[None, :, None, :]
        z = jnp.einsum('becn,beco->bno', combine, o)
        x_mlp2, x_attn2 = (z[..., :C], z[..., C:])
        return x + x_mlp2 + x_attn2
    h = _L0_tok_ref(x, L0_tok_w, L0_tok_b)
    h = h + _L0_attn_ref(_layernorm(h, axis=-1), L0_attn_Wq, L0_attn_Wk, L0_attn_Wv, L0_attn_Wo, L0_attn_proj)
    h = h + _L0_ffn_ref(_layernorm(h, axis=-1), L0_ffn_w_router, L0_ffn_gamma1, L0_ffn_beta1, L0_ffn_w1, L0_ffn_b1, L0_ffn_w2, L0_ffn_b2)
    return h

_drawn_inputs = setup_inputs


def setup_inputs(seed=0):
    import zlib

    import numpy as np

    out = dict(_drawn_inputs(seed))
    spreads = {'L0_ffn_gamma1': (1.0, 0.6),
     'L0_ffn_beta1': (0.0, 0.8),
     'L0_ffn_b1': (0.0, 0.351),
     'L0_ffn_b2': (0.0, 0.346)}
    factors = {}
    for name, (base, spread) in spreads.items():
        noise = np.random.default_rng([zlib.crc32(name.encode()), seed]).standard_normal(out[name].shape)
        drawn = base * np.exp(spread * noise) if base else spread * noise
        out[name] = jnp.asarray(drawn.astype(out[name].dtype))
    for name, factor in factors.items():
        out[name] = (out[name] * factor).astype(out[name].dtype)
    return out
```

```python
from contextlib import ExitStack

import concourse.bass as bass
from concourse import mybir

F32 = mybir.dt.float32
BF16 = mybir.dt.bfloat16
U32 = mybir.dt.uint32
ALU = mybir.AluOpType
ACT = mybir.ActivationFunctionType
AX = mybir.AxisListType
RMAX = bass.bass_isa.ReduceOp.max

B, N, C = 8, 750, 192
SP_P, SP_T = 125, 6
K = int(round(N * 0.7))
TP, TT = 105, 5
W2C = 263
KP = 2 * W2C
H, DH, M = 12, 16, 64
CH = 96
SK = 6 * DH
NPART = 3
PART_A = (0, 0, 0, 1, 1, 2)
PART_B = (0, 1, 2, 0, 1, 0)
E = 4
CAP = int(0.5 * K)
HID = 4 * C
FC1 = HID + 3 * C
BANDS = ((0, 24), (24, 48), (48, 96), (96, 192))
TINY = -(2.0 ** -126)
GH = 4
NG = H // GH
PAIRW = 2 * M


JOBS = (
    ["xT", "xT4", "q0", "q1", "k0", "k1", "v", "v4", "ss"] + [f"mq{t}" for t in range(TT)]
    + [f"mk{t}" for t in range(TT)] + ["shift"] + [f"fk{t}" for t in range(TT)] + [f"fq{p}" for p in range(H // 2)]
    + ["ctx", "ctxT"] + [f"nd{g}" for g in range(NG)] + [f"ndT{t}" for t in range(TT)]
    + ["aT", "aT4", "wo", "wo4", "yT", "yT4", "Q0", "Q1", "K0", "K1", "V", "V4"] + [f"g{f}" for f in range(HID // 128)]
)
LATE = [f"NdT{t}" for t in range(TT)] + ["AT", "AT4"] + [f"z{t}" for t in range(TT)]
PLAN = {name: (i % 4, i // 4 + 1) for i, name in enumerate(JOBS + LATE)}
NS = 20 * NG
OFF = 28
PV_LAG = 2
ROWS_AT = (24, 44, 64)


def rows_item(g):
    return 2 * min(ROWS_AT[g] + 1, NS) + g




def tower(nc, x, tok_w, tok_b, wq, wk, wv, wo, projT, wr, gamma, beta, w1T, b1, w2T, b2, out):
    ctx = ExitStack()
    with ctx:
        def sb(name, shape, dt=F32):
            return ctx.enter_context(nc.sbuf_tensor(name, shape, dt))

        def sem(name):
            return ctx.enter_context(nc.semaphore(name))

        ps = ctx.enter_context(nc.psum_tensor("ps", [128, 8, 512], F32))
        sorted_x = nc.dram_tensor("sorted_x", [B * N, C], F32).ap()
        score_row = nc.dram_tensor("score_row", [1, N], F32).ap()
        prob_row = nc.dram_tensor("prob_row", [1, K * E], F32).ap()
        part_d = [nc.dram_tensor(f"part_d{i}", [NPART, C, KP], BF16).ap() for i in range(4)]

        ident = sb("ident", [128, 128])
        ident_b = sb("ident_b", [128, 128], BF16)
        head_of = sb("head_of", [CH, 2, H])
        neg_half = sb("neg_half", [TP, TT])
        wq_s, wk_s, wv_s, wo_s = (sb(f"w{n}_s", [CH, 2, C]) for n in "qkvo")
        w1_s = sb("w1_s", [CH + 1, 2, FC1])
        w2h_s = sb("w2h_s", [128, HID // 128, C])
        w2a_s = sb("w2a_s", [CH, 2, C])
        b2_s = sb("b2_s", [TP, C])
        gamma_s = sb("gamma_s", [TP, C])
        beta_s = sb("beta_s", [TP, C])
        wr_s = sb("wr_s", [TP, E, C])
        pj = sb("pj", [DH, M])
        pj_r = sb("pj_r", [DH, 2, M])
        pj_b = sb("pj_b", [DH, NPART, M], BF16)
        proj_k = sb("proj_k", [SK + NPART, M], BF16)
        tie = sb("tie", [TP, TT, K], BF16)

        s = {}
        for name in ("setup", "w_in", "w_half", "pj_out", "chain_p", "chain_v", "x_in", "score", "score_out", "row_in",
                     "rank"):
            s[name] = sem("s_" + name)
        once = [s[n] for n in s]
        scattered = sem("scattered")

        with nc.sbuf_tensor("w2h_in", [128, HID // 128, 2 * C], F32) as w2h_in, \
                nc.sbuf_tensor("w2a_in", [CH, 2, 2 * C], F32) as w2a_in, \
                nc.sbuf_tensor("b2_in", [TP, 2 * C], F32) as b2_in, \
                nc.Block() as block:
            n_weights = 18

            @block.sync
            def _(sp):
                def load(dst, src):
                    sp.dma_start(dst, src).then_inc(s["w_in"], 16)

                load(pj[:, :], projT)
                for dst, src in ((wq_s, wq), (wk_s, wk), (wv_s, wv), (wo_s, wo)):
                    load(dst[:, :, :], src.rearrange("(k p) n -> p k n", k=2))
                load(w1_s[0:CH, :, :], w1T.rearrange("(k p) n -> p k n", k=2))
                load(w1_s[CH:CH + 1, 1, :], b1)
                load(w2h_in[:, :, :], w2T[0:HID, :].rearrange("(k p) n -> p k n", p=128))
                load(w2a_in[:, :, :], w2T[HID:, :].rearrange("(k p) n -> p k n", k=2))
                load(b2_in[:, :], b2.to_broadcast([TP, 2 * C]))
                load(gamma_s[:, :], gamma.to_broadcast([TP, C]))
                load(beta_s[:, :], beta.to_broadcast([TP, C]))
                for e in range(E):
                    load(wr_s[:, e, :], wr[e:e + 1, :].to_broadcast([TP, C]))
                sp.wait_ge(s["setup"], 1)
                for i, part in enumerate(PART_B):
                    sp.dma_start(proj_k[DH * i:DH * (i + 1), :], pj_b[:, part, :]).then_inc(s["pj_out"], 16)
                sp.wait_ge(s["pj_out"], 16 * len(PART_B))
                sp.wait_ge(s["w_in"], 16 * 16)

            @block.gpsimd
            def _(pool):
                n = 0

                def link(ins):
                    nonlocal n
                    n += 1
                    ins.then_inc(s["chain_p"], 1)
                    pool.wait_ge(s["chain_p"], n)

                link(pool.memset(ident[:, :], 0.0))
                link(pool.affine_select(out=ident[:, :], in_=ident[:, :], compare_op=ALU.not_equal, fill=1.0,
                                        base=0, pattern=[[-1, 128]], channel_multiplier=1))
                link(pool.tensor_copy(ident_b[:, :], ident[:, :]))
                link(pool.memset(head_of[:, :, :], 1.0))
                link(pool.affine_select(out=head_of[:, :, :], in_=head_of[:, :, :], compare_op=ALU.is_ge, fill=0.0,
                                        base=0, pattern=[[CH, 2], [-DH, H]], channel_multiplier=1))
                link(pool.affine_select(out=head_of[:, :, :], in_=head_of[:, :, :], compare_op=ALU.is_ge, fill=0.0,
                                        base=DH - 1, pattern=[[-CH, 2], [DH, H]], channel_multiplier=-1))
                link(pool.memset(neg_half[:, :], -0.5))
                link(pool.memset(tie[:, :, :], TINY))
                link(pool.affine_select(out=tie[:, :, :], in_=tie[:, :, :], compare_op=ALU.is_gt, fill=0.0,
                                        base=0, pattern=[[1, TT], [-1, K]], channel_multiplier=TT))

            @block.vector
            def _(dve):
                n = 0

                def link(ins):
                    nonlocal n
                    n += 1
                    ins.then_inc(s["chain_v"], 1)
                    dve.wait_ge(s["chain_v"], n)

                link(dve.memset(proj_k[SK:SK + NPART, :], 1.0))
                dve.wait_ge(s["w_in"], 16 * 16)
                link(dve.tensor_copy(pj_b[:, 0, :], pj[:, :]))
                link(dve.tensor_tensor(pj_r[:, 0, :], pj[:, :], pj_b[:, 0, :], ALU.subtract))
                link(dve.tensor_copy(pj_b[:, 1, :], pj_r[:, 0, :]))
                dve.tensor_tensor(pj_b[:, 2, :], pj_r[:, 0, :], pj_b[:, 1, :], ALU.subtract).then_inc(s["setup"], 1)
                link(dve.tensor_tensor(w2h_s[:, :, :], w2h_in[:, :, 0:C], w2h_in[:, :, C:], ALU.add))
                link(dve.tensor_tensor(w2a_s[:, :, :], w2a_in[:, :, 0:C], w2a_in[:, :, C:], ALU.add))
                link(dve.tensor_tensor(b2_s[:, :], b2_in[:, 0:C], b2_in[:, C:], ALU.add))
        nc.all_engine_barrier()
        nc.all_engine_barrier(sems_to_clear=range(once[0].num, once[-1].num + 1))

        with ExitStack() as inner:
            def sbi(name, shape, dt=F32):
                return inner.enter_context(nc.sbuf_tensor(name, shape, dt))

            xs = sbi("xs", [SP_P, SP_T, C])
            tw = sbi("tw", [SP_P, C])
            tb = sbi("tb", [SP_P, 1])
            prod = sbi("prod", [SP_P, C])
            score = sbi("score", [SP_P, SP_T])
            score_b = sbi("score_b", [SP_P, SP_T])
            row = sbi("row", [SP_P, N])
            above = sbi("above", [SP_P, N], BF16)
            rank = sbi("rank", [SP_P, SP_T])
            target = sbi("target", [SP_P, SP_T], U32)
            base = sbi("base", [SP_P, 1])
            tie_s = sbi("tie_s", [SP_P, SP_T, N], BF16)
            with nc.Block() as block:
                @block.sync
                def _(sp):
                    sp.dma_start(tw[:, :], tok_w.to_broadcast([SP_P, C])).then_inc(s["w_in"], 16)
                    sp.dma_start(tb[:, :], tok_b.to_broadcast([SP_P, 1])).then_inc(s["w_in"], 16)
                    sp.wait_ge(s["w_in"], 32)

                @block.vector
                def _(dve):
                    dve.memset(base[:, :], 0.0).then_inc(s["chain_v"], 1)
                    dve.wait_ge(s["chain_v"], 1)

                @block.gpsimd
                def _(pool):
                    pool.memset(tie_s[:, :, :], TINY).then_inc(s["chain_p"], 1)
                    pool.wait_ge(s["chain_p"], 1)
                    pool.affine_select(out=tie_s[:, :, :], in_=tie_s[:, :, :], compare_op=ALU.is_gt, fill=0.0,
                                       base=0, pattern=[[1, SP_T], [-1, N]],
                                       channel_multiplier=SP_T).then_inc(s["chain_p"], 1)
                    pool.wait_ge(s["chain_p"], 2)
            nc.all_engine_barrier(sems_to_clear=range(once[0].num, once[-1].num + 1))

            with nc.Fori(0, B) as b:
                with nc.Block() as block:
                    @block.sync
                    def _(sp):
                        sp.dma_start(xs[:, :, :], x[b].rearrange("(p t) d -> p t d", t=SP_T)).then_inc(s["x_in"], 16)
                        sp.wait_ge(s["score"], 1)
                        sp.dma_start(score_row.rearrange("a (p t) -> (a p) t", t=SP_T),
                                     score_b[:, :]).then_inc(s["score_out"], 16)
                        sp.wait_ge(s["score_out"], 16)
                        sp.dma_start(row[:, :], score_row.to_broadcast([SP_P, N])).then_inc(s["row_in"], 16)

                    @block.vector
                    def _(dve):
                        n = 0

                        def link(ins):
                            nonlocal n
                            n += 1
                            ins.then_inc(s["chain_v"], 1)
                            dve.wait_ge(s["chain_v"], n)

                        dve.wait_ge(s["x_in"], 16)
                        for t in range(SP_T):
                            link(dve.tensor_tensor_reduce(prod[:, :], xs[:, t, :], tw[:, :], 1.0, 0.0, ALU.mult,
                                                          ALU.add, score[:, t:t + 1]))
                        dve.tensor_scalar(score_b[:, :], score[:, :], tb[:, 0:1], None,
                                          ALU.add).then_inc(s["score"], 1)
                        dve.wait_ge(s["score"], 1)
                        dve.wait_ge(s["row_in"], 16)
                        for t in range(SP_T):
                            link(dve.scalar_tensor_tensor(out=above[:, :], in0=row[:, :], scalar=score_b[:, t:t + 1],
                                                          in1=tie_s[:, t, :], op0=ALU.subtract, op1=ALU.is_gt,
                                                          accum_out=rank[:, t:t + 1]))
                        dve.tensor_scalar(target[:, :], rank[:, :], base[:, 0:1], None,
                                          ALU.add).then_inc(s["rank"], 1)
                        dve.wait_ge(s["rank"], 1)
                        link(dve.tensor_scalar(base[:, :], base[:, :], float(N), None, ALU.add))

                    @block.gpsimd
                    def _(pool):
                        pool.wait_ge(s["rank"], 1)
                        for t in range(SP_T):
                            pool.indirect_dma_start(sorted_x, bass.IndirectOffsetOnAxis(ap=target[:, t:t + 1], axis=0),
                                                    xs[:, t, :], None).then_inc(scattered, 16)
                        pool.wait_ge(scattered, b * (16 * SP_T) + 16 * SP_T)
                nc.all_engine_barrier(sems_to_clear=range(once[0].num, once[-1].num + 1))


        tok = sb("tok", [TP, TT, C])
        st = sb("st", [TP, 3, TT, 6])
        mv = sb("mv", [TP, 3, TT, 2])
        var_e = sb("var_e", [TP, 3, TT])
        rstd = sb("rstd", [TP, 3, TT])
        xn = sb("xn", [TP, TT, C])
        xT = sb("xT", [CH, 2, KP])
        part = [sb(f"part{i}", [CH, NPART, 2, KP], BF16) for i in range(2)]
        left = [sb(f"left{i}", [CH, 2, KP]) for i in range(2)]
        sq = sb("sq", [CH, 2, 2, KP])
        pq = sb("pq", [SK + NPART, H, KP], BF16)
        pk = sb("pk", [SK + NPART, H, KP], BF16)
        vp = sb("vp", [TP, TT, H, 2 * DH])
        squares = sb("squares", [TP, 2, TT, H])
        top = sb("top", [TP, 2, TT, H])
        top_k = sb("top_k", [TP, 2, H])
        shift = sb("shift", [TP, 2, TT, H])
        sh_l = sb("sh_l", [TP, 2, TT, H])
        sh_p = sb("sh_p", [TP, TT, 2, NPART, H], BF16)
        sh_row = sb("sh_row", [2 * NPART * H, KP], BF16)
        fk_pT = sb("fk_pT", [TP, 2 * GH * KP])
        fk = fk_pT[:, 0:TT * H * M].rearrange("p (t f) -> p t f", t=TT)
        pT = fk_pT[:, :].rearrange("p (r j c) -> p r j c", r=2, j=GH)
        fq = sb("fq", [PAIRW, H // 2, KP])
        cT = sb("cT", [128, NG, PAIRW])
        ctx_d = sb("ctx_d", [128, NG, 128])
        nd = sb("nd", [128, NG, KP])
        den = sb("den", [TP, TT, H])
        at = sb("at", [TP, TT, C])
        aT = sb("aT", [CH, 2, KP])
        h1 = sb("h1", [TP, TT, C])
        u = sb("u", [TP, TT, C])
        y = sb("y", [TP, TT, C])
        ym = sb("ym", [TP, TT, C + 1])
        yT = sb("yT", [CH + 1, 2, KP])
        lg = sb("lg", [TP, TT, E])
        lg_s = sb("lg_s", [TP, 4, TT])
        pr = sb("pr", [TP, 3, TT, E])
        prow = sb("prow", [TP, K, E])
        above2 = sb("above2", [TP, K], BF16)
        prod2 = sb("prod2", [TP, C])
        rank2 = sb("rank2", [TP, TT, E])
        chosen = sb("chosen", [TP, E, TT])
        gate = sb("gate", [TP, E, TT])
        apart, aleft = part, left
        sa, sk, va = pq, pk, vp
        nda, ata, aTa = nd, at, aT
        mxh = sb("mxh", [TP, H, TT, 2])
        rows = sb("rows", [NPART * GH, NG, KP], BF16)
        neg = sb("neg", [TP, NG, 2, TT, GH])
        neg_p = sb("neg_p", [TP, NG, TT, NPART, GH], BF16)
        gT, z, res = fq, xn, y

        names = ("tok_in var1 var2 var3 rstd1 rstd2 rstd3 xn sq hi_a mid mid_a lo lo_a scr scr_a stack stack_a top top_all "
                 "shift_parts shift_in eps_k eps_q blocks u y logits exps prob prob_out prob_in ym res stored "
                 "neg_parts neg_in s1_ready s1_free s2_ready s2_free p_used pv_free chain ones").split()
        q = {n: sem("q_" + n) for n in names}
        ready = [sem(f"q_ps_ready{i}") for i in range(4)]
        free = [sem(f"q_ps_free{i}") for i in range(4)]
        every = range(q[names[0]].num, free[-1].num + 1)

        def bank(name):
            return 2 * PLAN[name][0]

        def filled(eng, name):
            eng.wait_ge(ready[PLAN[name][0]], PLAN[name][1])

        def taken(eng, name):
            eng.wait_ge(free[PLAN[name][0]], PLAN[name][1])

        def taken_all(eng, some):
            for name in some:
                taken(eng, name)

        def takes(ins, name):
            ins.then_inc(free[PLAN[name][0]], 1)

        def cols(t):
            return slice(t * TP, (t + 1) * TP)

        def halves(name, m=CH):
            return ps[0:m, bank(name):bank(name) + 2, 0:W2C]

        def wide(name):
            return ps[0:TP, bank(name):bank(name) + 2, :].rearrange("p a c -> p (a c)")[:, 0:H * M]

        def tile_of(name, name4, t):
            k = bank(name) if t < TT - 1 else bank(name4)
            return ps[0:TP, k + t // 2 % 2, C * (t % 2):C * (t % 2 + 1)]

        def split2(ap):
            return ap.rearrange("p (a c) -> p a c", a=2)

        with nc.Block() as block:
            @block.vector
            def _(dve):
                dve.memset(vp[:, :, :, DH:], 1.0).then_inc(q["chain"], 1)
                dve.memset(sh_row[:, :], 0.0).then_inc(q["chain"], 1)
                dve.memset(rows[:, :, :], 0.0).then_inc(q["chain"], 1)
                dve.memset(xT[:, :, K:], 0.0).then_inc(q["chain"], 1)
                dve.memset(yT[:, :, K:], 0.0).then_inc(q["chain"], 1)
                dve.memset(ctx_d[:, :, :], 0.0).then_inc(q["chain"], 1)
                dve.wait_ge(q["chain"], 6)
        nc.all_engine_barrier(sems_to_clear=every)

        with nc.Fori(0, B) as b:
            with nc.Block() as block:
                @block.sync
                def _(sp):
                    sp.dma_start(tok[:, :, :], sorted_x.rearrange("(b n) d -> b n d", b=B)[b, 0:K, :].rearrange(
                        "(p t) d -> p t d", t=TT)).then_inc(q["tok_in"], 16)

                    def spread(src, low, low_n, dram, out_sem, out_n, dst, order, in_sem):
                        sp.wait_ge(q[low], low_n)
                        for k in range(NPART):
                            sp.dma_start(dram[k].rearrange("(g p) c -> p g c", g=2),
                                         src[:, k, :, :]).then_inc(q[out_sem], 16)
                        sp.wait_ge(q[out_sem], 16 * NPART * out_n)
                        for i, k in enumerate(order):
                            sp.dma_start(dst[DH * i:DH * (i + 1), :, :],
                                         dram[k].rearrange("(h d) c -> d h c", d=DH)).then_inc(q[in_sem], 16)

                    spread(part[0], "lo", 2, part_d[0], "scr", 1, pq, PART_A, "stack")
                    spread(part[1], "lo", 4, part_d[1], "scr", 2, pk, PART_A, "stack")
                    taken(sp, "shift")
                    for i, dst in enumerate((pq, pk)):
                        for k in range(NPART):
                            r = (i * NPART + k) * H
                            sp.dma_start(dst[SK + k:SK + k + 1, :, :], sh_row[r:r + H, :]).then_inc(q["shift_in"], 16)
                    sp.wait_ge(q["prob"], 1)
                    sp.dma_start(prob_row.rearrange("a (p t) -> (a p) t", t=TT * E),
                                 pr[:, 2, :, :].rearrange("p t e -> p (t e)")).then_inc(q["prob_out"], 16)
                    sp.wait_ge(q["prob_out"], 16)
                    sp.dma_start(prow[:, :, :].rearrange("p k e -> p (k e)"),
                                 prob_row.to_broadcast([TP, K * E])).then_inc(q["prob_in"], 16)
                    spread(apart[0], "lo_a", 2, part_d[2], "scr_a", 1, sa, PART_A, "stack_a")
                    spread(apart[1], "lo_a", 4, part_d[3], "scr_a", 2, sk, PART_B, "stack_a")
                    for g in range(NG):
                        sp.wait_ge(q["s1_free"], rows_item(g) + 1)
                        for k in range(NPART):
                            sp.dma_start(sa[SK + k:SK + k + 1, GH * g:GH * (g + 1), :],
                                         rows[GH * k:GH * (k + 1), g, :]).then_inc(q["neg_in"], 16)
                    sp.wait_ge(q["res"], 1)
                    sp.dma_start(out[b].rearrange("(p t) d -> p t d", t=TT), res[:, :, :]).then_inc(q["stored"], 16)
                    sp.wait_ge(q["stored"], 16)

                @block.tensor
                def _(pe):
                    def begin(name):
                        r, n = PLAN[name]
                        if n > 1:
                            pe.wait_ge(free[r], n - 1)
                        return 2 * r

                    def end(ins, name):
                        ins.then_inc(ready[PLAN[name][0]], 1)

                    def turn(name, name4, src, more=0):
                        k = begin(name)
                        for t in range(TT - 1):
                            for g in range(2):
                                m = CH + (more if g else 0)
                                ins = pe.transpose(ps[0:m, k + g, cols(t)], src[:, t, CH * g:CH * g + m],
                                                   ident[0:TP, 0:TP])
                        end(ins, name)
                        k = begin(name4)
                        for g in range(2):
                            m = CH + (more if g else 0)
                            ins = pe.transpose(ps[0:m, k + g, 0:TP], src[:, TT - 1, CH * g:CH * g + m],
                                               ident[0:TP, 0:TP])
                        end(ins, name4)

                    def project(name, w, c0, m, src, more=0):
                        k = begin(name)
                        for i in range(2):
                            for g in range(2):
                                kk = CH + (more if g else 0)
                                ins = pe.matmul(ps[0:m, k + i, 0:W2C], w[0:kk, g, c0:c0 + m],
                                                src[0:kk, g, W2C * i:W2C * (i + 1)], start=(g == 0), stop=(g == 1))
                        end(ins, name)

                    def project_rows(name, name4, w, c0, src, more=0):
                        begin(name)
                        for t in range(TT):
                            if t == TT - 1:
                                end(ins, name)
                                begin(name4)
                            for g in range(2):
                                kk = CH + (more if g else 0)
                                ins = pe.matmul(tile_of(name, name4, t), src[0:kk, g, cols(t)], w[0:kk, g, c0:c0 + C],
                                                start=(g == 0), stop=(g == 1))
                        end(ins, name4)

                    pe.wait_ge(q["xn"], TT)
                    turn("xT", "xT4", xn)
                    taken(pe, "xT")
                    taken(pe, "xT4")
                    for pre, w in (("q", wq_s), ("k", wk_s)):
                        for g in range(2):
                            project(f"{pre}{g}", w, CH * g, CH, xT)
                    project_rows("v", "v4", wv_s, 0, xT)
                    k = begin("ss")
                    pe.wait_ge(q["sq"], 4)
                    for i in range(2):
                        for t in range(TT):
                            for g in range(2):
                                ins = pe.matmul(ps[0:TP, k, (i * TT + t) * H:(i * TT + t + 1) * H],
                                                sq[:, i, g, cols(t)], head_of[:, g, :], start=(g == 0), stop=(g == 1))
                    end(ins, "ss")
                    for i, (src, pre) in enumerate(((pq, "mq"), (pk, "mk"))):
                        pe.wait_ge(q["stack"], 16 * 6 * (i + 1))
                        for t in range(TT):
                            k = begin(f"{pre}{t}")
                            for h in range(H):
                                ins = pe.matmul(ps[0:TP, k + h // 8, M * (h % 8):M * (h % 8 + 1)],
                                                src[0:SK, h, cols(t)], proj_k[0:SK, :], start=True, stop=True)
                            end(ins, f"{pre}{t}")
                    k = begin("shift")
                    pe.wait_ge(q["shift_parts"], 1)
                    for t in range(TT):
                        ins = pe.transpose(ps[0:2 * NPART * H, k, :].bitcast(BF16)[:, 106 * t:106 * t + TP],
                                           sh_p[:, t, :, :, :].rearrange("p i k h -> p (i k h)"), ident_b[0:TP, 0:TP])
                    end(ins, "shift")
                    pe.wait_ge(q["shift_in"], 16 * 2 * NPART)
                    for t in range(TT):
                        k = begin(f"fk{t}")
                        for h in range(H):
                            ins = pe.matmul(ps[0:TP, k + h // 8, M * (h % 8):M * (h % 8 + 1)],
                                            pk[:, h, cols(t)], proj_k[:, :], start=True, stop=True)
                        end(ins, f"fk{t}")
                    for p in range(H // 2):
                        k = begin(f"fq{p}")
                        for i in range(2):
                            for j in range(2):
                                ins = pe.matmul(ps[M * j:M * (j + 1), k + i, 0:W2C], proj_k[:, :],
                                                pq[:, 2 * p + j, W2C * i:W2C * (i + 1)], start=True, stop=True)
                        end(ins, f"fq{p}")
                    k = begin("ctx")
                    taken(pe, "v4")
                    pe.wait_ge(q["eps_k"], TT)
                    for g in range(NG):
                        for t in range(TT):
                            for j in range(GH):
                                h = GH * g + j
                                ins = pe.matmul(ps[32 * j:32 * (j + 1), k, PAIRW * g:PAIRW * (g + 1)],
                                                vp[:, t, h, :], fk[:, t, PAIRW * (h // 2):PAIRW * (h // 2 + 1)],
                                                start=(t == 0), stop=(t == TT - 1))
                    end(ins, "ctx")
                    k = begin("ctxT")
                    taken(pe, "ctx")
                    for g in range(NG):
                        ins = pe.transpose(ps[:, k, 128 * g:128 * (g + 1)], cT[:, g, :], ident[:, :])
                    end(ins, "ctxT")
                    taken(pe, "ctxT")
                    pe.wait_ge(q["eps_q"], H // 2)
                    for g in range(NG):
                        k = begin(f"nd{g}")
                        for i in range(2):
                            for j in range(2):
                                ins = pe.matmul(ps[M * j:M * (j + 1), k + i, 0:W2C], ctx_d[:, g, M * j:M * (j + 1)],
                                                fq[:, 2 * g + j, W2C * i:W2C * (i + 1)], start=True, stop=True)
                        end(ins, f"nd{g}")

                    def turn_nd(pre, src):
                        for t in range(TT):
                            k = begin(f"{pre}{t}")
                            for g in range(NG):
                                ins = pe.transpose(ps[0:TP, k, 128 * g:128 * (g + 1)], src[:, g, cols(t)],
                                                   ident[:, :])
                            end(ins, f"{pre}{t}")

                    taken_all(pe, [f"nd{g}" for g in range(NG)])
                    turn_nd("ndT", nd)
                    taken_all(pe, [f"ndT{t}" for t in range(TT)])
                    turn("aT", "aT4", at)
                    taken_all(pe, ["aT", "aT4"])
                    project_rows("wo", "wo4", wo_s, 0, aT)

                    pe.wait_ge(q["ym"], len(BANDS) + 1)
                    turn("yT", "yT4", ym, 1)
                    taken_all(pe, ["yT", "yT4"])
                    for i, pre in enumerate("QK"):
                        for g in range(2):
                            project(f"{pre}{g}", w1_s, HID + C * i + CH * g, CH, yT, 1)
                    project_rows("V", "V4", w1_s, HID + 2 * C, yT, 1)
                    for f in range(HID // 128):
                        project(f"g{f}", w1_s, 128 * f, 128, yT, 1)

                    taken_all(pe, JOBS[-4:])
                    pe.wait_ge(q["stack_a"], 16 * 6 * 2)
                    pe.wait_ge(q["ones"], 1)

                    item = 0

                    def first(i):
                        nonlocal item
                        h, t = GH * (i // 20) + i % GH, i % 20 // GH
                        for half in range(2):
                            if item >= 2:
                                pe.wait_ge(q["s1_free"], item - 1)
                            n = W2C - half
                            pe.matmul(ps[0:TP, 6 + item % 2, 0:n], sa[0:SK, h, cols(t)],
                                      sk[0:SK, h, W2C * half:W2C * half + n],
                                      start=True, stop=True).then_inc(q["s1_ready"], 1)
                            item += 1

                    def first_rows(g):
                        nonlocal item
                        assert item == rows_item(g)
                        pe.wait_ge(q["s1_free"], item - 1)
                        pe.wait_ge(q["neg_parts"], g + 1)
                        for t in range(TT):
                            ins = pe.transpose(ps[0:NPART * GH, 6 + item % 2, :].bitcast(BF16)[:, 106 * t:106 * t + TP],
                                               neg_p[:, g, t, :, :].rearrange("p k h -> p (k h)"),
                                               ident_b[0:TP, 0:TP])
                        ins.then_inc(q["s1_ready"], 1)
                        item += 1

                    def second(i):
                        h, t = GH * (i // 20) + i % GH, i % 20 // GH
                        if i % 20 == 0:
                            pe.wait_ge(q["neg_in"], 16 * NPART * (i // 20 + 1))
                        if i >= 2:
                            pe.wait_ge(q["s2_free"], i - 1)
                        for half in range(2):
                            ins = pe.matmul(ps[0:TP, 2 * (i % 2) + half, 0:W2C], sk[:, h, cols(t)],
                                            sa[:, h, W2C * half:W2C * (half + 1)], start=True, stop=True)
                        ins.then_inc(q["s2_ready"], 1)

                    def weigh(n):
                        g, t = n // TT, n % TT
                        pe.wait_ge(q["s2_free"], GH * (n + 1))
                        if t == 0 and g:
                            pe.wait_ge(q["pv_free"], g)
                        for half in range(2):
                            for j in range(GH):
                                ins = pe.matmul(ps[32 * j:32 * (j + 1), 4 + half, 0:W2C], va[:, t, GH * g + j, :],
                                                pT[:, n % 2, j, W2C * half:W2C * (half + 1)],
                                                start=(t == 0), stop=(t == TT - 1))
                        ins.then_inc(q["p_used"], 1)

                    for step in range(NS + OFF + PV_LAG + 1):
                        if step < NS:
                            first(step)
                        if step in ROWS_AT:
                            first_rows(ROWS_AT.index(step))
                        i = step - OFF
                        if 0 <= i < NS:
                            second(i)
                        n = i - PV_LAG - GH + 1
                        if n >= 0 and n % GH == 0:
                            weigh(n // GH)

                    pe.wait_ge(q["pv_free"], NG)
                    pe.wait_ge(q["s1_free"], item)
                    pe.wait_ge(q["s2_free"], NS)
                    turn_nd("NdT", nda)
                    taken_all(pe, [f"NdT{t}" for t in range(TT)])
                    turn("AT", "AT4", ata)
                    taken_all(pe, ["AT", "AT4"])
                    for t in range(TT):
                        k = begin(f"z{t}")
                        for f in range(HID // 128):
                            pe.matmul(ps[0:TP, k, 0:C], gT[:, f, cols(t)], w2h_s[:, f, :], start=(f == 0), stop=False)
                        for g in range(2):
                            ins = pe.matmul(ps[0:TP, k, 0:C], aTa[:, g, cols(t)], w2a_s[:, g, :],
                                            start=False, stop=(g == 1))
                        end(ins, f"z{t}")

                @block.scalar
                def _(act):
                    def out_of(name, dst, src, func=ACT.Copy, scale=1.0):
                        filled(act, name)
                        takes(act.activation(dst, src, func, scale=scale), name)

                    def turned(name, name4, dst):
                        out_of(name, dst[:, :, 0:4 * TP], ps[0:CH, bank(name):bank(name) + 2, 0:4 * TP])
                        out_of(name4, dst[:, :, 4 * TP:K], ps[0:CH, bank(name4):bank(name4) + 2, 0:TP])

                    def values(name, name4, dst):
                        filled(act, name)
                        for i in range(2):
                            ins = act.activation(dst[:, 2 * i:2 * i + 2, :, 0:DH],
                                                 ps[0:TP, bank(name) + i, 0:2 * C].rearrange(
                                                     "p (t h d) -> p t h d", t=2, h=H), ACT.Copy)
                        takes(ins, name)
                        out_of(name4, dst[:, 4, :, 0:DH],
                               ps[0:TP, bank(name4), 0:C].rearrange("p (h d) -> p h d", h=H))

                    turned("xT", "xT4", xT)
                    for i, pre in enumerate("qk"):
                        for g in range(2):
                            filled(act, f"{pre}{g}")
                            act.activation(split2(part[i][:, 0, g, :]), halves(f"{pre}{g}"), ACT.Copy)
                            act.activation(split2(sq[:, i, g, :]), halves(f"{pre}{g}"),
                                           ACT.Square).then_inc(q["sq"], 1)
                    values("v", "v4", vp)
                    out_of("ss", squares[:, :, :, :].rearrange("p i t h -> p (i t h)"),
                           ps[0:TP, bank("ss"), 0:2 * TT * H])
                    out_of("shift", sh_row[:, 0:K].rearrange("p (t c) -> p t c", t=TT),
                           ps[0:2 * NPART * H, bank("shift"), :].bitcast(BF16)[:, 0:106 * TT].rearrange(
                               "p (t c) -> p t c", t=TT)[:, :, 0:TP])
                    for t in range(TT):
                        out_of(f"fk{t}", fk[:, t, :], wide(f"fk{t}"), ACT.Exp, DH ** -0.25)
                    for p in range(H // 2):
                        out_of(f"fq{p}", split2(fq[:, p, :]), halves(f"fq{p}", 128), ACT.Exp, DH ** -0.25)
                    out_of("ctx", cT[:, :, :].rearrange("p g c -> p (g c)"), ps[:, bank("ctx"), 0:NG * PAIRW])
                    for g in range(NG):
                        out_of(f"nd{g}", split2(nd[:, g, :]), halves(f"nd{g}", 128))
                    turned("aT", "aT4", aT)
                    act.wait_ge(q["logits"], 1)
                    act.activation(pr[:, 0, :, :], pr[:, 1, :, :], ACT.Exp).then_inc(q["exps"], 1)

                    for name, c in (("yT", slice(0, 4 * TP)), ("yT4", slice(4 * TP, K))):
                        filled(act, name)
                        n = c.stop - c.start
                        act.activation(yT[0:CH, 0, c], ps[0:CH, bank(name), 0:n], ACT.Copy)
                        takes(act.activation(yT[:, 1, c], ps[0:CH + 1, bank(name) + 1, 0:n], ACT.Copy), name)
                    for i, pre in enumerate("QK"):
                        for g in range(2):
                            filled(act, f"{pre}{g}")
                            act.activation(split2(apart[i][:, 0, g, :]), halves(f"{pre}{g}"),
                                           ACT.Copy).then_inc(q["hi_a"], 1)
                    values("V", "V4", va)
                    for f in range(HID // 128):
                        out_of(f"g{f}", split2(gT[:, f, :]), halves(f"g{f}", 128), ACT.Gelu)

                    def gathered(g):
                        act.wait_ge(q["p_used"], TT * (g + 1))
                        act.activation(split2(nda[:, g, :]), ps[:, 4:6, 0:W2C], ACT.Copy).then_inc(q["pv_free"], 1)

                    for i in range(NS):
                        n = i // GH
                        act.wait_ge(q["s2_ready"], i + 1)
                        if n >= 2:
                            act.wait_ge(q["p_used"], n - 1)
                        act.activation(split2(pT[:, n % 2, i % GH, :]), ps[0:TP, 2 * (i % 2):2 * (i % 2) + 2, 0:W2C],
                                       ACT.Exp, scale=DH ** -0.5).then_inc(q["s2_free"], 1)
                        if i >= 20 and i % 20 == 4:
                            gathered(i // 20 - 1)
                    gathered(NG - 1)
                    turned("AT", "AT4", aTa)

                @block.gpsimd
                def _(pool):
                    def inverse_root(i):
                        pool.wait_ge(q[f"var{i + 1}"], 1)
                        pool.tensor_tensor(rstd[:, i, :], var_e[:, i, :], neg_half[:, :],
                                           ALU.pow).then_inc(q[f"rstd{i + 1}"], 1)

                    def low_parts(p, rest, mid, lo):
                        for i in range(4):
                            pool.wait_ge(q[mid], i + 1)
                            pool.tensor_tensor(p[i // 2][:, 2, i % 2, :], rest[i // 2][:, i % 2, :],
                                               p[i // 2][:, 1, i % 2, :], ALU.subtract).then_inc(q[lo], 1)

                    inverse_root(0)
                    low_parts(part, left, "mid", "lo")
                    pool.wait_ge(q["top"], 1)
                    pool.partition_all_reduce(top_k[:, 1, :], top_k[:, 0, :], TP, RMAX).then_inc(q["top_all"], 1)
                    inverse_root(1)
                    inverse_root(2)
                    low_parts(apart, aleft, "mid_a", "lo_a")

                @block.vector
                def _(dve):
                    n = 0

                    def go(ins):
                        nonlocal n
                        n += 1
                        ins.then_inc(q["chain"], 1)

                    def settle():
                        dve.wait_ge(q["chain"], n)

                    def link(ins):
                        go(ins)
                        settle()

                    def statistics(src, i, eps, signal):
                        for t in range(TT):
                            go(dve.bn_stats(st[:, i, t, :], src[:, t, :]))
                        settle()
                        for t in range(TT):
                            go(dve.bn_aggr(mv[:, i, t, :], st[:, i, t, :]))
                        settle()
                        dve.tensor_scalar(var_e[:, i, :], mv[:, i, :, 1], eps, None, ALU.add).then_inc(q[signal], 1)

                    def normalized(dst, src, i, signal):
                        dve.wait_ge(q[f"rstd{i + 1}"], 1)
                        for t in range(TT):
                            dve.tensor_scalar(dst[:, t, :], src[:, t, :], mv[:, i, t, 0:1], rstd[:, i, t:t + 1],
                                              ALU.subtract, ALU.mult).then_inc(q[signal], 1)

                    def lower_parts(names_, p, rest, high, mid):
                        for k, name in enumerate(names_):
                            i, g = k // 2, k % 2
                            dve.wait_ge(q[high], k + 1)
                            takes(dve.tensor_tensor(split2(rest[i][:, g, :]), halves(name),
                                                    split2(p[i][:, 0, g, :]), ALU.subtract), name)
                            taken(dve, name)
                            dve.tensor_copy(p[i][:, 1, g, :], rest[i][:, g, :]).then_inc(q[mid], 1)

                    dve.wait_ge(q["tok_in"], 16)
                    statistics(tok, 0, 1e-5, "var1")
                    normalized(xn, tok, 0, "xn")
                    lower_parts(("q0", "q1", "k0", "k1"), part, left, "sq", "mid")
                    for i, pre in enumerate(("mq", "mk")):
                        for t in range(TT):
                            filled(dve, f"{pre}{t}")
                            takes(dve.tensor_reduce(top[:, i, t, :],
                                                    wide(f"{pre}{t}").rearrange("p (h m) -> p h m", m=M), AX.X,
                                                    ALU.max), f"{pre}{t}")
                    taken_all(dve, [f"{pre}{t}" for pre in ("mq", "mk") for t in range(TT)])
                    dve.tensor_reduce(top_k[:, 0, :], top[:, 1, :, :].rearrange("p t h -> p h t"), AX.X,
                                      ALU.max).then_inc(q["top"], 1)
                    taken(dve, "ss")
                    go(dve.scalar_tensor_tensor(out=shift[:, 0, :, :], in0=squares[:, 0, :, :], scalar=-0.25,
                                                in1=top[:, 0, :, :], op0=ALU.mult, op1=ALU.subtract))
                    dve.wait_ge(q["top_all"], 1)
                    link(dve.scalar_tensor_tensor(
                        out=shift[:, 1, :, :], in0=squares[:, 1, :, :], scalar=-0.25,
                        in1=top_k[:, 1, :].unsqueeze(1).to_broadcast([TP, TT, H]),
                        op0=ALU.mult, op1=ALU.subtract))
                    for i in range(2):
                        p = [sh_p[:, :, i, k, :] for k in range(NPART)]
                        link(dve.tensor_copy(p[0], shift[:, i, :, :]))
                        link(dve.tensor_tensor(sh_l[:, i, :, :], shift[:, i, :, :], p[0], ALU.subtract))
                        link(dve.tensor_copy(p[1], sh_l[:, i, :, :]))
                        ins = dve.tensor_tensor(p[2], sh_l[:, i, :, :], p[1], ALU.subtract)
                        if i == 0:
                            go(ins)
                        else:
                            ins.then_inc(q["shift_parts"], 1)
                    for t in range(TT):
                        taken(dve, f"fk{t}")
                        dve.tensor_scalar(fk[:, t, :], fk[:, t, :], 1e-4, None, ALU.add).then_inc(q["eps_k"], 1)
                    for p in range(H // 2):
                        taken(dve, f"fq{p}")
                        dve.tensor_scalar(fq[:, p, :], fq[:, p, :], 1e-4, None, ALU.add).then_inc(q["eps_q"], 1)
                    filled(dve, "ctxT")
                    src = ps[:, bank("ctxT"), 0:NG * 128].rearrange("p (g j c) -> p g j c", j=2, c=2 * DH)
                    dst = ctx_d[:, :, :].rearrange("p g c -> p (g c)").rearrange("p (g j c) -> p g j c", j=2, c=2 * DH)
                    dve.tensor_copy(dst[0:M, :, 0, :], src[0:M, :, 0, :])
                    takes(dve.tensor_copy(dst[M:, :, 1, :], src[M:, :, 1, :]), "ctxT")

                    def divided(pre, dst):
                        for t in range(TT):
                            filled(dve, f"{pre}{t}")
                            v = ps[0:TP, bank(f"{pre}{t}"), 0:NG * 128].rearrange("p (h c) -> p h c", c=2 * DH)
                            link(dve.reciprocal(den[:, t, :], v[:, :, DH]))
                            takes(dve.tensor_tensor(dst[:, t, :].rearrange("p (h d) -> p h d", d=DH), v[:, :, 0:DH],
                                                    den[:, t, :].unsqueeze(2).to_broadcast([TP, H, DH]), ALU.mult),
                                  f"{pre}{t}")

                    divided("ndT", at)
                    for t in range(TT):
                        name = "wo" if t < TT - 1 else "wo4"
                        filled(dve, name)
                        ins = dve.tensor_tensor(h1[:, t, :], tok[:, t, :], tile_of("wo", "wo4", t), ALU.add)
                        if t >= TT - 2:
                            takes(ins, name)
                    taken_all(dve, ["wo", "wo4"])
                    statistics(h1, 1, 1e-5, "var2")
                    normalized(u, h1, 1, "u")
                    dve.wait_ge(q["u"], TT)
                    statistics(u, 2, 1e-6, "var3")
                    for t in range(TT):
                        for e in range(E):
                            link(dve.tensor_tensor_reduce(prod2[:, :], u[:, t, :], wr_s[:, e, :], 1.0, 0.0, ALU.mult,
                                                          ALU.add, lg[:, t, e:e + 1]))
                    link(dve.tensor_reduce(lg_s[:, 0, :], lg[:, :, :], AX.X, ALU.max))
                    dve.tensor_tensor(pr[:, 1, :, :], lg[:, :, :],
                                      lg_s[:, 0, :].unsqueeze(2).to_broadcast([TP, TT, E]),
                                      ALU.subtract).then_inc(q["logits"], 1)
                    normalized(y, u, 2, "y")
                    dve.wait_ge(q["y"], TT)
                    dve.wait_ge(q["exps"], 1)
                    link(dve.tensor_reduce(lg_s[:, 1, :], pr[:, 0, :, :], AX.X, ALU.add))
                    link(dve.reciprocal(lg_s[:, 2, :], lg_s[:, 1, :]))
                    dve.tensor_tensor(pr[:, 2, :, :], pr[:, 0, :, :],
                                      lg_s[:, 2, :].unsqueeze(2).to_broadcast([TP, TT, E]),
                                      ALU.mult).then_inc(q["prob"], 1)
                    link(dve.tensor_tensor(y[:, :, :], y[:, :, :],
                                           gamma_s[:, :].unsqueeze(1).to_broadcast([TP, TT, C]), ALU.mult))
                    link(dve.tensor_tensor(y[:, :, :], y[:, :, :],
                                           beta_s[:, :].unsqueeze(1).to_broadcast([TP, TT, C]), ALU.add))
                    dve.wait_ge(q["prob"], 1)
                    dve.wait_ge(q["prob_in"], 16)
                    for t in range(TT):
                        for e in range(E):
                            link(dve.scalar_tensor_tensor(out=above2[:, :], in0=prow[:, :, e],
                                                          scalar=pr[:, 2, t, e:e + 1], in1=tie[:, t, :],
                                                          op0=ALU.subtract, op1=ALU.is_gt,
                                                          accum_out=rank2[:, t, e:e + 1]))
                    link(dve.tensor_scalar(chosen[:, :, :], rank2[:, :, :].rearrange("p t e -> p e t"), float(CAP),
                                           None, ALU.is_lt))
                    link(dve.tensor_tensor(gate[:, :, :], chosen[:, :, :],
                                           pr[:, 2, :, :].rearrange("p t e -> p e t"), ALU.mult))
                    for e in range(E - 2, -1, -1):
                        link(dve.tensor_tensor(chosen[:, e, :], chosen[:, e, :], chosen[:, e + 1, :], ALU.add))
                        link(dve.tensor_tensor(gate[:, e, :], gate[:, e, :], gate[:, e + 1, :], ALU.add))
                    for e, (lo, hi) in enumerate(BANDS):
                        dve.tensor_tensor(ym[:, :, lo:hi], y[:, :, lo:hi],
                                          chosen[:, e, :].unsqueeze(2).to_broadcast([TP, TT, hi - lo]),
                                          ALU.mult).then_inc(q["ym"], 1)
                    dve.tensor_copy(ym[:, :, C:], chosen[:, 0, :].unsqueeze(2)).then_inc(q["ym"], 1)
                    go(dve.tensor_tensor(h1[:, :, :], u[:, :, :], h1[:, :, :], ALU.add))

                    lower_parts(("Q0", "Q1", "K0", "K1"), apart, aleft, "hi_a", "mid_a")
                    dve.memset(sk[SK:, :, :], 1.0).then_inc(q["ones"], 1)

                    item = 0
                    for step in range(ROWS_AT[-1] + 1):
                        if step < NS:
                            h, t = GH * (step // 20) + step % GH, step % 20 // GH
                            for half in range(2):
                                dve.wait_ge(q["s1_ready"], item + 1)
                                dve.tensor_reduce(mxh[:, h, t, half:half + 1], ps[0:TP, 6 + item % 2, 0:W2C - half],
                                                  AX.X, ALU.max).then_inc(q["s1_free"], 1)
                                item += 1
                        if step % 20 == 19 and step < NS:
                            g = step // 20
                            dve.wait_ge(q["s1_free"], item)
                            r0, r1 = neg[:, g, 0, :, :], neg[:, g, 1, :, :]
                            p = [neg_p[:, g, :, k, :] for k in range(NPART)]
                            link(dve.tensor_reduce(r0, mxh[:, GH * g:GH * (g + 1), :, :].rearrange("p h t a -> p t h a"),
                                                   AX.X, ALU.max, negate=True))
                            link(dve.tensor_copy(p[0], r0))
                            link(dve.tensor_tensor(r1, r0, p[0], ALU.subtract))
                            link(dve.tensor_copy(p[1], r1))
                            dve.tensor_tensor(p[2], r1, p[1], ALU.subtract).then_inc(q["neg_parts"], 1)
                        if step in ROWS_AT:
                            dve.wait_ge(q["s1_ready"], item + 1)
                            dve.tensor_copy(rows[:, ROWS_AT.index(step), 0:K].rearrange("p (t c) -> p t c", t=TT),
                                            ps[0:NPART * GH, 6 + item % 2, :].bitcast(BF16)[:, 0:106 * TT].rearrange(
                                                "p (t c) -> p t c", t=TT)[:, :, 0:TP]).then_inc(q["s1_free"], 1)
                            item += 1

                    divided("NdT", ata)
                    for t in range(TT):
                        filled(dve, f"z{t}")
                        takes(dve.tensor_tensor(z[:, t, :], ps[0:TP, bank(f"z{t}"), 0:C], b2_s[:, :], ALU.add), f"z{t}")
                    taken_all(dve, [f"z{t}" for t in range(TT)])
                    for e, (lo, hi) in enumerate(BANDS):
                        go(dve.tensor_tensor(z[:, :, lo:hi], z[:, :, lo:hi],
                                             gate[:, e, :].unsqueeze(2).to_broadcast([TP, TT, hi - lo]), ALU.mult))
                    settle()
                    dve.tensor_tensor(res[:, :, :], z[:, :, :], h1[:, :, :], ALU.add).then_inc(q["res"], 1)
            nc.all_engine_barrier(sems_to_clear=every)


def kernel(x, L0_tok_w, L0_tok_b, L0_attn_Wq, L0_attn_Wk, L0_attn_Wv, L0_attn_Wo, L0_attn_proj, L0_ffn_w_router,
           L0_ffn_gamma1, L0_ffn_beta1, L0_ffn_w1, L0_ffn_b1, L0_ffn_w2, L0_ffn_b2):
    import numpy as np
    import concourse.bacc as bacc
    from concourse.bass_utils import run_bass_kernel_spmd

    nc = bacc.Bacc("TRN2", target_bir_lowering=False, num_devices=1)
    laid = {
        "x": x, "tok_w": np.asarray(L0_tok_w).reshape(1, C), "tok_b": np.asarray(L0_tok_b).reshape(1, 1),
        "wq": L0_attn_Wq, "wk": L0_attn_Wk, "wv": L0_attn_Wv, "wo": L0_attn_Wo,
        "projT": np.asarray(L0_attn_proj).T, "wr": L0_ffn_w_router,
        "gamma": np.asarray(L0_ffn_gamma1).reshape(1, C), "beta": np.asarray(L0_ffn_beta1).reshape(1, C),
        "w1T": np.asarray(L0_ffn_w1).T, "b1": np.asarray(L0_ffn_b1).reshape(1, FC1),
        "w2T": np.asarray(L0_ffn_w2).T, "b2": np.asarray(L0_ffn_b2).reshape(1, 2 * C),
    }
    arrays = {f"in_{name}": np.ascontiguousarray(a) for name, a in laid.items()}
    aps = [nc.dram_tensor(name, a.shape, mybir.dt.from_np(a.dtype), kind="ExternalInput").ap()
           for name, a in arrays.items()]
    out = nc.dram_tensor("out_0", (B, K, C), F32, kind="ExternalOutput").ap()
    tower(nc, *aps, out)
    r = run_bass_kernel_spmd(nc, [arrays], core_ids=[0])
    return r.results[0]["out_0"]
```

```python
from contextlib import ExitStack

import concourse.bass as bass
from concourse import mybir

F32 = mybir.dt.float32
BF16 = mybir.dt.bfloat16
U32 = mybir.dt.uint32
ALU = mybir.AluOpType
ACT = mybir.ActivationFunctionType
AX = mybir.AxisListType
RMAX = bass.bass_isa.ReduceOp.max

B, N, C = 8, 750, 192
SP_P, SP_T = 125, 6
K = int(round(N * 0.7))
TP, TT = 105, 5
W2C = 263
KP = 2 * W2C
H, DH, M = 12, 16, 64
CH = 96
NPART = 3
PART_A = (0, 0, 0, 1, 1, 2, 1)
PART_B = (0, 1, 2, 0, 1, 0, 2)
BLOCKS = len(PART_A)
SK = BLOCKS * DH
ONES_FROM = 96
E = 4
CAP = int(0.5 * K)
HID = 4 * C
FC1 = HID + 3 * C
BANDS = ((0, 24), (24, 48), (48, 96), (96, 192))
TINY = -(2.0 ** -126)
GH = 4
NG = H // GH
UNREAD = 2
PAIRW = 2 * M


JOBS_A = (
    ["xT", "xT4", "q0", "q1", "k0", "k1", "v", "v4", "ss"] + [f"mq{t}" for t in range(TT)]
    + [f"mk{t}" for t in range(TT)] + ["shift"] + [f"fk{t}" for t in range(TT)] + [f"fq{p}" for p in range(H // 2)]
    + ["ctx", "ctxT"] + [f"nd{g}" for g in range(NG)] + [f"ndT{t}" for t in range(TT)] + ["aT", "aT4", "wo", "wo4"]
)
EARLY_B = ["yT", "yT4", "Q0", "Q1", "K0", "K1", "V", "V4"] + [f"g{f}" for f in range(HID // 128)]
LATE_B = [f"NdT{t}" for t in range(TT)] + ["AT", "AT4"] + [f"z{t}" for t in range(TT)]
GUESTS = [f"m{i}{t}" for i in "qk" for t in range(TT)][1::2]
FIRST_BANK = (0, 2, 4, 6, 4)
PLAN = {name: (3, i + 1) for i, name in enumerate(j for j in JOBS_A if j not in GUESTS)}
PLAN |= {name: (4, i + 1) for i, name in enumerate(GUESTS)}
PLAN |= {name: (i % 3, i // 3 + 1) for i, name in enumerate(EARLY_B + LATE_B)}
PV_BANK = 4
NS = 20 * NG
OFF = 28
PV_LAG = 2
ROWS_AT = (24, 44, 64)
PRE = len(EARLY_B)
ATT = PRE + NS + OFF + PV_LAG + 1


AT = {"ln1": 2.5, "xn": 3.5, "xT": 6, "xT4": 6.5, "q0": 7, "q1": 8, "k0": 9, "k1": 10, "v": 12, "v4": 13, "ss": 17, "top": 29, "shift": 34,
      "ctx": 53, "ctxT": 55, "aT": 64, "aT4": 65, "wo": 66, "wo4": 67, "ln2": 68, "u": 72, "ln3": 76,
      "router": 80, "prob": 88, "y": 88, "exps": 91, "ranks": 92, "ym": 112}
AT |= {f"mq{t}": 19 + t for t in range(TT)} | {f"mk{t}": 24 + t for t in range(TT)}
AT |= {f"fk{t}": 40 + t for t in range(TT)} | {f"fq{p}": 45 + p for p in range(H // 2)}
AT |= {f"nd{g}": 56 + g for g in range(NG)} | {f"ndT{t}": 59 + t for t in range(TT)}
SPREAD = {"norm": 0.5, "router": 1.5, "ranks": 2.5}


def attention_banks():
    bank, before, held, count = {}, {}, {}, {"s1": 0, "s2": 0}

    def item(kind, ring):
        key = (kind, count[kind])
        b = min(ring, key=lambda r: held.get(r, (-1, None))[0])
        bank[key], before[key] = b, held.get(b, (-1, None))[1]
        held[b] = (sum(count.values()), key)
        count[kind] += 1

    for step in range(NS + OFF):
        for _ in range(2 * (step < NS) + (step in ROWS_AT)):
            item("s1", range(4) if step < OFF - 2 else range(2))
        if step >= OFF:
            for _ in range(2):
                item("s2", range(4) if step > ROWS_AT[-1] else range(2, 4))
    return bank, before


def weave(*programs):
    due = [next(p, None) for p in programs]
    while any(d is not None for d in due):
        i = min((d, i) for i, d in enumerate(due) if d is not None)[1]
        due[i] = next(programs[i], None)


def rows_item(g):
    return 2 * min(ROWS_AT[g] + 1, NS) + g




def tower(nc, x, tok_w, tok_b, wq, wk, wv, wo, projT, wr, gamma, beta, w1T, b1, w2T, b2, out):
    ctx = ExitStack()
    with ctx:
        def sb(name, shape, dt=F32):
            return ctx.enter_context(nc.sbuf_tensor(name, shape, dt))

        def sem(name):
            return ctx.enter_context(nc.semaphore(name))

        ps = ctx.enter_context(nc.psum_tensor("ps", [128, 8, 512], F32))
        sorted_x = nc.dram_tensor("sorted_x", [B * N, C], F32).ap()
        score_row = nc.dram_tensor("score_row", [B, 1, N], F32).ap()
        prob_row = nc.dram_tensor("prob_row", [1, K * E], F32).ap()
        part_d = [nc.dram_tensor(f"part_d{i}", [NPART, C, KP], BF16).ap() for i in range(4)]

        ident = sb("ident", [128, 128])
        ident_b = sb("ident_b", [128, 128], BF16)
        head_of = sb("head_of", [CH, 2, H])
        neg_half = sb("neg_half", [TP, TT])
        wq_s, wk_s, wv_s, wo_s = (sb(f"w{n}_s", [CH, 2, C]) for n in "qkvo")
        w1_s = sb("w1_s", [CH + 1, 2, FC1])
        w2h_s = sb("w2h_s", [128, HID // 128, C])
        w2a_s = sb("w2a_s", [CH, 2, C])
        b2_s = sb("b2_s", [TP, C])
        gamma_s = sb("gamma_s", [TP, C])
        beta_s = sb("beta_s", [TP, C])
        wr_s = sb("wr_s", [TP, E, C])
        pj = sb("pj", [DH, M])
        pj_r = sb("pj_r", [DH, 2, M])
        pj_b = sb("pj_b", [DH, NPART, M], BF16)
        proj_k = sb("proj_k", [SK + NPART, M], BF16)
        tie = sb("tie", [TP, TT, K], BF16)

        s = {}
        for name in ("setup", "ones", "w_in", "tok_w_in", "pj_out", "chain_p", "chain_v", "x_in0", "x_in1", "product",
                     "score", "score_out", "row_in0", "row_in1", "rank", "tie", "target"):
            s[name] = sem("s_" + name)
        once = [s[n] for n in s]
        scattered = sem("scattered")

        with ExitStack() as inner:
            def sbi(name, shape, dt=F32):
                return inner.enter_context(nc.sbuf_tensor(name, shape, dt))

            xs = sbi("xs", [SP_P, B, SP_T, C])
            tw = sbi("tw", [SP_P, C])
            tb = sbi("tb", [SP_P, 1])
            prod = sbi("prod", [SP_P, SP_T, C])
            score = sbi("score", [SP_P, B, SP_T])
            score_b = sbi("score_b", [SP_P, B, SP_T])
            row = sbi("row", [SP_P, B, N])
            above = sbi("above", [SP_P, SP_T, N], BF16)
            rank = sbi("rank", [SP_P, B, SP_T])
            base = sbi("base", [SP_P, B, SP_T])
            target = sbi("target", [SP_P, B, SP_T], U32)
            tie_s = sbi("tie_s", [SP_P, SP_T, N], BF16)
            w2h_in = sbi("w2h_in", [128, HID // 128, 2 * C])
            w2a_in = sbi("w2a_in", [CH, 2, 2 * C])
            b2_in = sbi("b2_in", [TP, 2 * C])
            with nc.Block() as block:
                @block.scalar
                def _(act):
                    act.dma_start(tw[:, :], tok_w.to_broadcast([SP_P, C])).then_inc(s["tok_w_in"], 16)
                    act.dma_start(tb[:, :], tok_b.to_broadcast([SP_P, 1])).then_inc(s["tok_w_in"], 16)

                    for b in range(B):
                        if b >= 2:
                            act.wait_ge(s[f"x_in{b % 2}"], 16 * (b // 2))
                        act.dma_start(xs[:, b, :, :],
                                      x[b].rearrange("(p t) d -> p t d", t=SP_T)).then_inc(s[f"x_in{b % 2}"], 16)

                @block.sync
                def _(sp):
                    def load(dst, src):
                        sp.dma_start(dst, src).then_inc(s["w_in"], 16)

                    load(pj[:, :], projT)
                    for dst, src in ((wq_s, wq), (wk_s, wk), (wv_s, wv), (wo_s, wo)):
                        load(dst[:, :, :], src.rearrange("(k p) n -> p k n", k=2))
                    load(w1_s[0:CH, :, :], w1T.rearrange("(k p) n -> p k n", k=2))
                    load(w1_s[CH:CH + 1, 1, :], b1)
                    load(w2h_in[:, :, :], w2T[0:HID, :].rearrange("(k p) n -> p k n", p=128))
                    load(w2a_in[:, :, :], w2T[HID:, :].rearrange("(k p) n -> p k n", k=2))
                    load(b2_in[:, :], b2.to_broadcast([TP, 2 * C]))
                    load(gamma_s[:, :], gamma.to_broadcast([TP, C]))
                    load(beta_s[:, :], beta.to_broadcast([TP, C]))
                    for e in range(E):
                        load(wr_s[:, e, :], wr[e:e + 1, :].to_broadcast([TP, C]))
                    for b in range(B):
                        sp.wait_ge(s["score"], b + 1)
                        sp.dma_start(score_row[b].rearrange("a (p t) -> (a p) t", t=SP_T),
                                     score_b[:, b, :]).then_inc(s["score_out"], 16)
                        sp.wait_ge(s["score_out"], 16 * (b + 1))
                        if b >= 2:
                            sp.wait_ge(s[f"row_in{b % 2}"], 16 * (b // 2))
                        sp.dma_start(row[:, b, :], score_row[b].to_broadcast([SP_P, N])).then_inc(
                            s[f"row_in{b % 2}"], 16)
                    sp.wait_ge(s["ones"], 1)
                    sp.wait_ge(s["setup"], 1)
                    for i, part in enumerate(PART_B):
                        sp.dma_start(proj_k[DH * i:DH * (i + 1), :], pj_b[:, part, :]).then_inc(s["pj_out"], 16)
                    sp.wait_ge(s["pj_out"], 16 * len(PART_B))
                    sp.wait_ge(s["w_in"], 16 * 16)

                @block.vector
                def _(dve):
                    dve.wait_ge(s["tok_w_in"], 32)

                    def scores(b):
                        dve.wait_ge(s[f"x_in{b % 2}"], 16 * (b // 2 + 1))
                        for t in range(SP_T):
                            if b:
                                dve.wait_ge(s["product"], (b - 1) * SP_T + t + 1)
                            dve.tensor_tensor_reduce(prod[:, t, :], xs[:, b, t, :], tw[:, :], 1.0, 0.0, ALU.mult, ALU.add,
                                                     score[:, b, t:t + 1]).then_inc(s["product"], 1)
                        dve.wait_ge(s["product"], (b + 1) * SP_T)
                        dve.tensor_scalar(score_b[:, b, :], score[:, b, :], tb[:, 0:1], None,
                                          ALU.add).then_inc(s["score"], 1)

                    def ranks(b):
                        if b == 0:
                            dve.wait_ge(s["tie"], 2 + B)
                        dve.wait_ge(s["score"], b + 1)
                        dve.wait_ge(s[f"row_in{b % 2}"], 16 * (b // 2 + 1))
                        for t in range(SP_T):
                            if b:
                                dve.wait_ge(s["rank"], (b - 1) * SP_T + t + 1)
                            dve.scalar_tensor_tensor(out=above[:, t, :], in0=row[:, b, :],
                                                     scalar=score_b[:, b, t:t + 1], in1=tie_s[:, t, :],
                                                     op0=ALU.subtract, op1=ALU.is_gt,
                                                     accum_out=rank[:, b, t:t + 1]).then_inc(s["rank"], 1)
                        dve.wait_ge(s["rank"], (b + 1) * SP_T)
                        dve.tensor_tensor(target[:, b, :], rank[:, b, :], base[:, b, :],
                                          ALU.add).then_inc(s["target"], 1)

                    for b in range(B + 2):
                        if b < B:
                            scores(b)
                        if b >= 2:
                            ranks(b - 2)
                    n = 0

                    def link(ins):
                        nonlocal n
                        n += 1
                        ins.then_inc(s["chain_v"], 1)
                        dve.wait_ge(s["chain_v"], n)

                    dve.memset(proj_k[ONES_FROM:, :], 1.0).then_inc(s["ones"], 1)
                    dve.wait_ge(s["w_in"], 16 * 16)
                    link(dve.tensor_copy(pj_b[:, 0, :], pj[:, :]))
                    link(dve.tensor_tensor(pj_r[:, 0, :], pj[:, :], pj_b[:, 0, :], ALU.subtract))
                    link(dve.tensor_copy(pj_b[:, 1, :], pj_r[:, 0, :]))
                    dve.tensor_tensor(pj_b[:, 2, :], pj_r[:, 0, :], pj_b[:, 1, :], ALU.subtract).then_inc(s["setup"], 1)
                    link(dve.tensor_tensor(w2h_s[:, :, :], w2h_in[:, :, 0:C], w2h_in[:, :, C:], ALU.add))
                    link(dve.tensor_tensor(w2a_s[:, :, :], w2a_in[:, :, 0:C], w2a_in[:, :, C:], ALU.add))
                    link(dve.tensor_tensor(b2_s[:, :], b2_in[:, 0:C], b2_in[:, C:], ALU.add))

                @block.gpsimd
                def _(pool):
                    pool.memset(tie_s[:, :, :], TINY).then_inc(s["tie"], 1)
                    pool.wait_ge(s["tie"], 1)
                    pool.affine_select(out=tie_s[:, :, :], in_=tie_s[:, :, :], compare_op=ALU.is_gt, fill=0.0,
                                       base=0, pattern=[[1, SP_T], [-1, N]],
                                       channel_multiplier=SP_T).then_inc(s["tie"], 1)
                    for i in range(B):
                        pool.memset(base[:, i, :], float(N * i)).then_inc(s["tie"], 1)
                    n = 0

                    def link(ins):
                        nonlocal n
                        n += 1
                        ins.then_inc(s["chain_p"], 1)
                        pool.wait_ge(s["chain_p"], n)

                    link(pool.memset(ident[:, :], 0.0))
                    link(pool.affine_select(out=ident[:, :], in_=ident[:, :], compare_op=ALU.not_equal, fill=1.0,
                                            base=0, pattern=[[-1, 128]], channel_multiplier=1))
                    link(pool.tensor_copy(ident_b[:, :], ident[:, :]))
                    link(pool.memset(head_of[:, :, :], 1.0))
                    link(pool.affine_select(out=head_of[:, :, :], in_=head_of[:, :, :], compare_op=ALU.is_ge, fill=0.0,
                                            base=0, pattern=[[CH, 2], [-DH, H]], channel_multiplier=1))
                    link(pool.affine_select(out=head_of[:, :, :], in_=head_of[:, :, :], compare_op=ALU.is_ge, fill=0.0,
                                            base=DH - 1, pattern=[[-CH, 2], [DH, H]], channel_multiplier=-1))
                    link(pool.memset(neg_half[:, :], -0.5))
                    link(pool.memset(tie[:, :, :], TINY))
                    link(pool.affine_select(out=tie[:, :, :], in_=tie[:, :, :], compare_op=ALU.is_gt, fill=0.0,
                                            base=0, pattern=[[1, TT], [-1, K]], channel_multiplier=TT))
                    for b in range(B):
                        pool.wait_ge(s["target"], b + 1)
                        for t in range(SP_T):
                            pool.indirect_dma_start(sorted_x,
                                                    bass.IndirectOffsetOnAxis(ap=target[:, b, t:t + 1], axis=0),
                                                    xs[:, b, t, :], None).then_inc(scattered, 16)
                    pool.wait_ge(scattered, 16 * SP_T * B)
            nc.all_engine_barrier(sems_to_clear=range(once[0].num, once[-1].num + 1))

        tok = sb("tok", [TP, TT, C])
        st = sb("st", [TP, 3, TT, 6])
        mv = sb("mv", [TP, 3, TT, 2])
        var_e = sb("var_e", [TP, 3, TT])
        rstd = sb("rstd", [TP, 3, TT])
        xn = sb("xn", [TP, TT, C])
        xT = sb("xT", [CH, 2, KP])
        work = sb("work", [128, 10 * KP])
        left = [work[0:CH, 2 * KP * i:2 * KP * (i + 1)].rearrange("p (g c) -> p g c", g=2) for i in range(2)]
        part = [work[0:CH, (4 + 3 * i) * KP:(7 + 3 * i) * KP].bitcast(BF16).rearrange(
            "p (k g c) -> p k g c", k=NPART, g=2) for i in range(2)]
        fq = work[:, 0:H // 2 * KP].rearrange("p (h c) -> p h c", c=KP)
        pq = sb("pq", [SK + NPART, H, KP], BF16)
        pk = sb("pk", [SK + NPART, H, KP], BF16)
        vp = sb("vp", [TP, TT, H, 2 * DH])
        squares = sb("squares", [TP, 2, TT, H])
        top = sb("top", [TP, 2, TT, H])
        top_k = sb("top_k", [TP, 2, H])
        shift = sb("shift", [TP, 2, TT, H])
        sh_l = sb("sh_l", [TP, 2, TT, H])
        sh_p = sb("sh_p", [TP, TT, 2, NPART, H], BF16)
        sh_row = sb("sh_row", [2 * NPART * H, KP], BF16)
        fk_nd = sb("fk_nd", [128, TT * H * M])
        sq = fk_nd[0:CH, 0:4 * KP].rearrange("p (i g c) -> p i g c", i=2, g=2)
        prow = fk_nd[0:TP, 0:K * E].rearrange("p (k e) -> p k e", e=E)
        fk = fk_nd[0:TP, :].rearrange("p (t f) -> p t f", t=TT)
        nd = fk_nd[:, 0:NG * KP].rearrange("p (g c) -> p g c", g=NG)
        cT = sb("cT", [128, NG, PAIRW])
        ctx_d = sb("ctx_d", [128, NG, 128])
        den = sb("den", [TP, 2, TT, H])
        u = sb("u", [TP, TT, C])
        ym = sb("ym", [TP, TT, C + 1])
        lg = sb("lg", [TP, TT, E])
        lg_s = sb("lg_s", [TP, 4, TT])
        pr = sb("pr", [TP, 3, TT, E])
        unread = sb("unread", [TP, UNREAD, W2C])
        rank2 = sb("rank2", [TP, TT, E])
        chosen = sb("chosen", [TP, E, TT])
        gate = sb("gate", [TP, E, TT])
        h1, at, y, aT = tok, xn, xn, xT

        yT_nd = sb("yT_nd", [128, NG, KP])
        yT = yT_nd[0:CH + 1, 0:2, :]
        ndb = yT_nd
        gT_w = sb("gT_w", [128, H // 2 * KP])
        gT = gT_w[:, :].rearrange("p (f c) -> p f c", c=KP)
        left_b = gT_w[0:CH, 0:2 * KP].rearrange("p (g c) -> p g c", g=2)
        part_b = gT_w[0:CH, 2 * KP:5 * KP].bitcast(BF16).rearrange("p (k g c) -> p k g c", k=NPART, g=2)
        sa = sb("sa", [SK + NPART, H, KP], BF16)
        sk = sb("sk", [SK + NPART, H, KP], BF16)
        va = sb("va", [TP, TT, H, 2 * DH])
        pT = sb("pT", [TP, 2, GH, KP])
        mxh = sb("mxh", [TP, H, TT, 2])
        neg = sb("neg", [TP, 2, TT, GH])
        neg_p = sb("neg_p", [TP, NG, TT, NPART, GH], BF16)
        rows = sb("rows", [NPART * GH, NG, KP], BF16)
        late = sa[0:TP, :, :].rearrange("p h c -> p (h c)").bitcast(F32)
        atb = late[:, 0:TT * C].rearrange("p (t c) -> p t c", t=TT)
        aTb = late[0:CH, TT * C:TT * C + 2 * KP].rearrange("p (g c) -> p g c", g=2)
        base_b = sb("base_b", [TP, TT, C])
        gate_b = sb("gate_b", [TP, E, TT])
        z = atb

        names = ("tok_in var1 var2 var3 rstd1 rstd2 rstd3 xn sq mid lo scr stack top top_all shift_parts shift_in eps_k "
                 "eps_q u y gamma beta logits exps prob prob_out prob_in ym chain "
                 "kept hi_b left_b mid_b lo_b scr_b stack_b ones neg_parts neg_in s1_ready s1_free s2_ready s2_free "
                 "p_used pv_free gated res stored").split()
        q = {n: sem("q_" + n) for n in names}
        ready = [sem(f"q_ps_ready{i}") for i in range(len(FIRST_BANK))]
        free = [sem(f"q_ps_free{i}") for i in range(len(FIRST_BANK))]
        every = range(q[names[0]].num, free[-1].num + 1)

        def bank(name):
            return FIRST_BANK[PLAN[name][0]]

        a_bank, a_before = attention_banks()

        def bank_free(pe, key):
            if key is not None:
                pe.wait_ge(q[key[0] + "_free"], key[1] + 1)

        def filled(eng, name):
            eng.wait_ge(ready[PLAN[name][0]], PLAN[name][1])

        def taken(eng, name):
            eng.wait_ge(free[PLAN[name][0]], PLAN[name][1])

        def taken_all(eng, some):
            for name in some:
                taken(eng, name)

        def takes(ins, name):
            ins.then_inc(free[PLAN[name][0]], 1)

        def cols(t):
            return slice(t * TP, (t + 1) * TP)

        def halves(name, m=CH):
            return ps[0:m, bank(name):bank(name) + 2, 0:W2C]

        def wide(name):
            return ps[0:TP, bank(name):bank(name) + 2, :].rearrange("p a c -> p (a c)")[:, 0:H * M]

        def tile_of(name, name4, t):
            k = bank(name) if t < TT - 1 else bank(name4)
            return ps[0:TP, k + t // 2 % 2, C * (t % 2):C * (t % 2 + 1)]

        def split2(ap):
            return ap.rearrange("p (a c) -> p a c", a=2)

        with nc.Block() as block:
            @block.vector
            def _(dve):
                dve.memset(sk[ONES_FROM:, :, :], 1.0).then_inc(q["chain"], 1)
                dve.memset(xT[:, :, K:], 0.0).then_inc(q["chain"], 1)
                dve.memset(ctx_d[:, :, :], 0.0).then_inc(q["chain"], 1)
                dve.wait_ge(q["chain"], 3)

            @block.gpsimd
            def _(pool):
                pool.memset(vp[:, :, :, DH:], 1.0).then_inc(q["kept"], 1)
                pool.memset(va[:, :, :, DH:], 1.0).then_inc(q["kept"], 1)
                pool.memset(sh_row[:, :], 0.0).then_inc(q["kept"], 1)
                pool.memset(rows[:, :, :], 0.0).then_inc(q["kept"], 1)
                pool.wait_ge(q["kept"], 4)
        nc.all_engine_barrier(sems_to_clear=every)

        def one_round(a, b, with_a, with_b):
            with nc.Block() as block:
                def run(programs_a, programs_b):
                    weave(*([programs_a()] if with_a else []), *([programs_b()] if with_b else []))

                @block.sync
                def _(sp):
                    def spread(src, low, low_n, dram, out_sem, out_n, dst, order, in_sem):
                        sp.wait_ge(q[low], low_n)
                        for k in range(NPART):
                            sp.dma_start(dram[k].rearrange("(g p) c -> p g c", g=2),
                                         src[:, k, :, :]).then_inc(q[out_sem], 16)
                        sp.wait_ge(q[out_sem], 16 * NPART * out_n)
                        for i, k in enumerate(order):
                            sp.dma_start(dst[DH * i:DH * (i + 1), :, :],
                                         dram[k].rearrange("(h d) c -> d h c", d=DH)).then_inc(q[in_sem], 16)

                    def pass_a():
                        yield 0
                        if with_b:
                            sp.wait_ge(q["kept"], 2)
                        sp.dma_start(tok[:, :, :], sorted_x.rearrange("(b n) d -> b n d", b=B)[a, 0:K, :].rearrange(
                            "(p t) d -> p t d", t=TT)).then_inc(q["tok_in"], 16)
                        yield AT["k0"]
                        spread(part[0], "lo", 2, part_d[0], "scr", 1, pq, PART_A, "stack")
                        yield AT["v"]
                        spread(part[1], "lo", 4, part_d[1], "scr", 2, pk, PART_A, "stack")
                        yield AT["shift"]
                        taken(sp, "shift")
                        for i, dst in enumerate((pq, pk)):
                            for k in range(NPART):
                                r = (i * NPART + k) * H
                                sp.dma_start(dst[SK + k:SK + k + 1, :, :],
                                             sh_row[r:r + H, :]).then_inc(q["shift_in"], 16)
                        yield AT["prob"]
                        sp.wait_ge(q["prob"], 1)
                        sp.dma_start(prob_row.rearrange("a (p t) -> (a p) t", t=TT * E),
                                     pr[:, 2, :, :].rearrange("p t e -> p (t e)")).then_inc(q["prob_out"], 16)
                        sp.wait_ge(q["prob_out"], 16)
                        sp.dma_start(fk_nd[0:TP, 0:K * E], prob_row.to_broadcast([TP, K * E])).then_inc(
                            q["prob_in"], 16)

                    def pass_b():
                        yield 4
                        spread(part_b, "lo_b", 2, part_d[2], "scr_b", 1, sa, PART_A, "stack_b")
                        yield 6
                        spread(part_b, "lo_b", 4, part_d[3], "scr_b", 2, sk, PART_B, "stack_b")
                        for g in range(NG):
                            yield PRE + ROWS_AT[g]
                            sp.wait_ge(q["s1_free"], rows_item(g) + 1)
                            for k in range(NPART):
                                sp.dma_start(sa[SK + k:SK + k + 1, GH * g:GH * (g + 1), :],
                                             rows[GH * k:GH * (k + 1), g, :]).then_inc(q["neg_in"], 16)
                        yield ATT + len(LATE_B)
                        sp.wait_ge(q["res"], TT * len(BANDS))
                        sp.dma_start(out[b].rearrange("(p t) d -> p t d", t=TT), atb[:, :, :]).then_inc(
                            q["stored"], 16)
                        sp.wait_ge(q["stored"], 16)

                    run(pass_a, pass_b)

                @block.tensor
                def _(pe):
                    def begin(name):
                        r, n = PLAN[name]
                        if n > 1:
                            pe.wait_ge(free[r], n - 1)
                        return bank(name)

                    def end(ins, name):
                        ins.then_inc(ready[PLAN[name][0]], 1)

                    def turn(name, src, more=0):
                        k = begin(name)
                        for t in ([TT - 1] if name.endswith("4") else range(TT - 1)):
                            for g in range(2):
                                m = CH + (more if g else 0)
                                ins = pe.transpose(ps[0:m, k + g, cols(t % (TT - 1))], src[:, t, CH * g:CH * g + m],
                                                   ident[0:TP, 0:TP])
                        end(ins, name)

                    def project(name, w, c0, m, src, more=0):
                        k = begin(name)
                        for i in range(2):
                            for g in range(2):
                                kk = CH + (more if g else 0)
                                ins = pe.matmul(ps[0:m, k + i, 0:W2C], w[0:kk, g, c0:c0 + m],
                                                src[0:kk, g, W2C * i:W2C * (i + 1)], start=(g == 0), stop=(g == 1))
                        end(ins, name)

                    def project_rows(name, w, c0, src, more=0):
                        begin(name)
                        for t in ([TT - 1] if name.endswith("4") else range(TT - 1)):
                            for g in range(2):
                                kk = CH + (more if g else 0)
                                ins = pe.matmul(tile_of(name, name, t), src[0:kk, g, cols(t)], w[0:kk, g, c0:c0 + C],
                                                start=(g == 0), stop=(g == 1))
                        end(ins, name)

                    def turn_nd(name, t, src):
                        k = begin(name)
                        for g in range(NG):
                            ins = pe.transpose(ps[0:TP, k, 128 * g:128 * (g + 1)], src[:, g, cols(t)], ident[:, :])
                        end(ins, name)

                    def features(name, src, depth, t):
                        k = begin(name)
                        for h in range(H):
                            ins = pe.matmul(ps[0:TP, k + h // 8, M * (h % 8):M * (h % 8 + 1)],
                                            src[0:depth, h, cols(t)], proj_k[0:depth, :], start=True, stop=True)
                        end(ins, name)

                    def pass_a():
                        yield AT["xT"]
                        pe.wait_ge(q["xn"], TT)
                        turn("xT", xn)
                        yield AT["xT4"]
                        turn("xT4", xn)
                        taken_all(pe, ["xT", "xT4"])
                        for pre, w in (("q", wq_s), ("k", wk_s)):
                            for g in range(2):
                                yield AT[f"{pre}{g}"]
                                project(f"{pre}{g}", w, CH * g, CH, xT)
                        for name in ("v", "v4"):
                            yield AT[name]
                            project_rows(name, wv_s, 0, xT)
                        yield AT["ss"]
                        k = begin("ss")
                        pe.wait_ge(q["sq"], 4)
                        for i in range(2):
                            for t in range(TT):
                                for g in range(2):
                                    ins = pe.matmul(ps[0:TP, k, (i * TT + t) * H:(i * TT + t + 1) * H],
                                                    sq[:, i, g, cols(t)], head_of[:, g, :],
                                                    start=(g == 0), stop=(g == 1))
                        end(ins, "ss")
                        for i, (src, pre) in enumerate(((pq, "mq"), (pk, "mk"))):
                            for t in range(TT):
                                yield AT[f"{pre}{t}"]
                                if f"{pre}{t}" == GUESTS[0] and with_b:
                                    taken_all(pe, EARLY_B[-3:])
                                if t == 0:
                                    pe.wait_ge(q["stack"], 16 * BLOCKS * (i + 1))
                                features(f"{pre}{t}", src, SK, t)
                        yield AT["shift"]
                        k = begin("shift")
                        pe.wait_ge(q["shift_parts"], 1)
                        for t in range(TT):
                            ins = pe.transpose(ps[0:2 * NPART * H, k, :].bitcast(BF16)[:, 106 * t:106 * t + TP],
                                               sh_p[:, t, :, :, :].rearrange("p i k h -> p (i k h)"),
                                               ident_b[0:TP, 0:TP])
                        end(ins, "shift")
                        for t in range(TT):
                            yield AT[f"fk{t}"]
                            if t == 0:
                                pe.wait_ge(q["shift_in"], 16 * 2 * NPART)
                            features(f"fk{t}", pk, SK + NPART, t)
                        for p in range(H // 2):
                            yield AT[f"fq{p}"]
                            k = begin(f"fq{p}")
                            for i in range(2):
                                for j in range(2):
                                    ins = pe.matmul(ps[M * j:M * (j + 1), k + i, 0:W2C], proj_k[:, :],
                                                    pq[:, 2 * p + j, W2C * i:W2C * (i + 1)], start=True, stop=True)
                            end(ins, f"fq{p}")
                        yield AT["ctx"]
                        k = begin("ctx")
                        taken(pe, "v4")
                        pe.wait_ge(q["eps_k"], TT)
                        for g in range(NG):
                            for t in range(TT):
                                for j in range(GH):
                                    h = GH * g + j
                                    ins = pe.matmul(ps[32 * j:32 * (j + 1), k, PAIRW * g:PAIRW * (g + 1)],
                                                    vp[:, t, h, :], fk[:, t, PAIRW * (h // 2):PAIRW * (h // 2 + 1)],
                                                    start=(t == 0), stop=(t == TT - 1))
                        end(ins, "ctx")
                        yield AT["ctxT"]
                        k = begin("ctxT")
                        taken(pe, "ctx")
                        for g in range(NG):
                            ins = pe.transpose(ps[:, k, 128 * g:128 * (g + 1)], cT[:, g, :], ident[:, :])
                        end(ins, "ctxT")
                        for g in range(NG):
                            yield AT[f"nd{g}"]
                            if g == 0:
                                taken(pe, "ctxT")
                            pe.wait_ge(q["eps_q"], 2 * (g + 1))
                            k = begin(f"nd{g}")
                            for i in range(2):
                                for j in range(2):
                                    ins = pe.matmul(ps[M * j:M * (j + 1), k + i, 0:W2C],
                                                    ctx_d[:, g, M * j:M * (j + 1)],
                                                    fq[:, 2 * g + j, W2C * i:W2C * (i + 1)], start=True, stop=True)
                            end(ins, f"nd{g}")
                        for t in range(TT):
                            yield AT[f"ndT{t}"]
                            if t == 0:
                                taken(pe, f"nd{NG - 1}")
                            turn_nd(f"ndT{t}", t, nd)
                        yield AT["aT"]
                        taken_all(pe, [f"ndT{t}" for t in range(TT)])
                        turn("aT", at)
                        yield AT["aT4"]
                        turn("aT4", at)
                        yield AT["wo"]
                        taken_all(pe, ["aT", "aT4"])
                        project_rows("wo", wo_s, 0, aT)
                        yield AT["wo4"]
                        project_rows("wo4", wo_s, 0, aT)

                    item = 0

                    def first(i):
                        nonlocal item
                        h, t = GH * (i // 20) + i % GH, i % 20 // GH
                        for half in range(2):
                            bank_free(pe, a_before["s1", item])
                            n = W2C - half
                            pe.matmul(ps[0:TP, a_bank["s1", item], 0:n], sa[0:SK, h, cols(t)],
                                      sk[0:SK, h, W2C * half:W2C * half + n],
                                      start=True, stop=True).then_inc(q["s1_ready"], 1)
                            item += 1

                    def first_rows(g):
                        nonlocal item
                        assert item == rows_item(g)
                        bank_free(pe, a_before["s1", item])
                        pe.wait_ge(q["neg_parts"], g + 1)
                        for t in range(TT):
                            ins = pe.transpose(
                                ps[0:NPART * GH, a_bank["s1", item], :].bitcast(BF16)[:, 106 * t:106 * t + TP],
                                neg_p[:, g, t, :, :].rearrange("p k h -> p (k h)"), ident_b[0:TP, 0:TP])
                        ins.then_inc(q["s1_ready"], 1)
                        item += 1

                    def second(i):
                        h, t = GH * (i // 20) + i % GH, i % 20 // GH
                        if i % 20 == 0:
                            pe.wait_ge(q["neg_in"], 16 * NPART * (i // 20 + 1))
                        for half in range(2):
                            bank_free(pe, a_before["s2", 2 * i + half])
                            pe.matmul(ps[0:TP, a_bank["s2", 2 * i + half], 0:W2C], sk[:, h, cols(t)],
                                      sa[:, h, W2C * half:W2C * (half + 1)],
                                      start=True, stop=True).then_inc(q["s2_ready"], 1)

                    def weigh(n):
                        g, t = n // TT, n % TT
                        pe.wait_ge(q["s2_free"], 2 * GH * (n + 1))
                        if n == 0 and with_a:
                            taken(pe, GUESTS[-1])
                        if t == 0 and g:
                            pe.wait_ge(q["pv_free"], g)
                        for half in range(2):
                            for j in range(GH):
                                ins = pe.matmul(ps[32 * j:32 * (j + 1), PV_BANK + half, 0:W2C],
                                                va[:, t, GH * g + j, :],
                                                pT[:, n % 2, j, W2C * half:W2C * (half + 1)],
                                                start=(t == 0), stop=(t == TT - 1))
                        ins.then_inc(q["p_used"], 1)

                    def pass_b():
                        yield 0
                        turn("yT", ym, 1)
                        yield 1
                        turn("yT4", ym, 1)
                        taken_all(pe, ["yT", "yT4"])
                        pe.wait_ge(q["ones"], 1)
                        for i, pre in enumerate("QK"):
                            for g in range(2):
                                yield 2 + 2 * i + g
                                project(f"{pre}{g}", w1_s, HID + C * i + CH * g, CH, yT, 1)
                        for i, name in enumerate(("V", "V4")):
                            yield 6 + i
                            project_rows(name, w1_s, HID + 2 * C, yT, 1)
                        for f in range(HID // 128):
                            yield 8 + f
                            project(f"g{f}", w1_s, 128 * f, 128, yT, 1)
                        yield PRE
                        taken_all(pe, EARLY_B[-3:])
                        pe.wait_ge(q["stack_b"], 16 * BLOCKS * 2)
                        for step in range(NS + OFF + PV_LAG + 1):
                            yield PRE + step
                            if step < NS:
                                first(step)
                            if step in ROWS_AT:
                                first_rows(ROWS_AT.index(step))
                            i = step - OFF
                            if 0 <= i < NS:
                                second(i)
                            n = i - PV_LAG - GH + 1
                            if n >= 0 and n % GH == 0:
                                weigh(n // GH)
                        pe.wait_ge(q["pv_free"], NG)
                        pe.wait_ge(q["s1_free"], item)
                        pe.wait_ge(q["s2_free"], 2 * NS)
                        for t in range(TT):
                            yield ATT + t
                            turn_nd(f"NdT{t}", t, ndb)
                        taken_all(pe, [f"NdT{t}" for t in range(TT)])
                        yield ATT + TT
                        turn("AT", atb)
                        yield ATT + TT + 1
                        turn("AT4", atb)
                        taken_all(pe, ["AT", "AT4"])
                        for t in range(TT):
                            yield ATT + TT + 2 + t
                            k = begin(f"z{t}")
                            for f in range(HID // 128):
                                pe.matmul(ps[0:TP, k, 0:C], gT[:, f, cols(t)], w2h_s[:, f, :],
                                          start=(f == 0), stop=False)
                            for g in range(2):
                                ins = pe.matmul(ps[0:TP, k, 0:C], aTb[:, g, cols(t)], w2a_s[:, g, :],
                                                start=False, stop=(g == 1))
                            end(ins, f"z{t}")

                    run(pass_a, pass_b)

                @block.scalar
                def _(act):
                    def out_of(name, dst, src, func=ACT.Copy, scale=1.0):
                        filled(act, name)
                        takes(act.activation(dst, src, func, scale=scale), name)

                    def turned(name, dst):
                        if name.endswith("4"):
                            out_of(name, dst[:, :, 4 * TP:K], ps[0:CH, bank(name):bank(name) + 2, 0:TP])
                        else:
                            out_of(name, dst[:, :, 0:4 * TP], ps[0:CH, bank(name):bank(name) + 2, 0:4 * TP])

                    def values(name, dst):
                        if name.endswith("4"):
                            out_of(name, dst[:, 4, :, 0:DH],
                                   ps[0:TP, bank(name), 0:C].rearrange("p (h d) -> p h d", h=H))
                            return
                        filled(act, name)
                        for i in range(2):
                            ins = act.activation(dst[:, 2 * i:2 * i + 2, :, 0:DH],
                                                 ps[0:TP, bank(name) + i, 0:2 * C].rearrange(
                                                     "p (t h d) -> p t h d", t=2, h=H), ACT.Copy)
                        takes(ins, name)

                    def pass_a():
                        for name in ("xT", "xT4"):
                            yield AT[name]
                            turned(name, xT)
                        for i, pre in enumerate("qk"):
                            for g in range(2):
                                yield AT[f"{pre}{g}"]
                                filled(act, f"{pre}{g}")
                                act.activation(split2(part[i][:, 0, g, :]), halves(f"{pre}{g}"), ACT.Copy)
                                act.activation(split2(sq[:, i, g, :]), halves(f"{pre}{g}"),
                                               ACT.Square).then_inc(q["sq"], 1)
                                taken(act, f"{pre}{g}")
                                act.activation(part[i][:, 1, g, :], left[i][:, g, :], ACT.Copy).then_inc(q["mid"], 1)
                        for name in ("v", "v4"):
                            yield AT[name]
                            values(name, vp)
                        yield AT["ss"]
                        out_of("ss", squares[:, :, :, :].rearrange("p i t h -> p (i t h)"),
                               ps[0:TP, bank("ss"), 0:2 * TT * H])
                        yield AT["shift"]
                        out_of("shift", sh_row[:, 0:K].rearrange("p (t c) -> p t c", t=TT),
                               ps[0:2 * NPART * H, bank("shift"), :].bitcast(BF16)[:, 0:106 * TT].rearrange(
                                   "p (t c) -> p t c", t=TT)[:, :, 0:TP])
                        for t in range(TT):
                            yield AT[f"fk{t}"]
                            out_of(f"fk{t}", fk[:, t, :], wide(f"fk{t}"), ACT.Exp, DH ** -0.25)
                        for p in range(H // 2):
                            yield AT[f"fq{p}"]
                            out_of(f"fq{p}", split2(fq[:, p, :]), halves(f"fq{p}", 128), ACT.Exp, DH ** -0.25)
                        yield AT["ctx"]
                        out_of("ctx", cT[:, :, :].rearrange("p g c -> p (g c)"), ps[:, bank("ctx"), 0:NG * PAIRW])
                        for g in range(NG):
                            yield AT[f"nd{g}"]
                            out_of(f"nd{g}", split2(nd[:, g, :]), halves(f"nd{g}", 128))
                        for name in ("aT", "aT4"):
                            yield AT[name]
                            turned(name, aT)
                        yield AT["prob"]
                        act.wait_ge(q["logits"], 1)
                        act.activation(pr[:, 0, :, :], pr[:, 1, :, :], ACT.Exp).then_inc(q["exps"], 1)

                    def gathered(g):
                        act.wait_ge(q["p_used"], TT * (g + 1))
                        act.activation(split2(ndb[:, g, :]), ps[:, PV_BANK:PV_BANK + 2, 0:W2C],
                                       ACT.Copy).then_inc(q["pv_free"], 1)

                    def pass_b():
                        for i, (name, c) in enumerate((("yT", slice(0, 4 * TP)), ("yT4", slice(4 * TP, K)))):
                            yield i
                            filled(act, name)
                            n = c.stop - c.start
                            act.activation(yT[0:CH, 0, c], ps[0:CH, bank(name), 0:n], ACT.Copy)
                            takes(act.activation(yT[:, 1, c], ps[0:CH + 1, bank(name) + 1, 0:n], ACT.Copy), name)
                        for i, pre in enumerate("QK"):
                            for g in range(2):
                                yield 2 + 2 * i + g
                                if i and g == 0:
                                    act.wait_ge(q["scr_b"], 16 * NPART)
                                filled(act, f"{pre}{g}")
                                act.activation(split2(part_b[:, 0, g, :]), halves(f"{pre}{g}"),
                                               ACT.Copy).then_inc(q["hi_b"], 1)
                                taken(act, f"{pre}{g}")
                                act.activation(part_b[:, 1, g, :], left_b[:, g, :], ACT.Copy).then_inc(q["mid_b"], 1)
                        for i, name in enumerate(("V", "V4")):
                            yield 6 + i
                            values(name, va)
                        for f in range(HID // 128):
                            yield 8 + f
                            if f == 0:
                                act.wait_ge(q["scr_b"], 2 * 16 * NPART)
                            out_of(f"g{f}", split2(gT[:, f, :]), halves(f"g{f}", 128), ACT.Gelu)
                        for i in range(NS):
                            yield PRE + OFF + i
                            n = i // GH
                            for half in range(2):
                                act.wait_ge(q["s2_ready"], 2 * i + half + 1)
                                if n >= 2 and half == 0:
                                    act.wait_ge(q["p_used"], n - 1)
                                act.activation(pT[:, n % 2, i % GH, W2C * half:W2C * (half + 1)],
                                               ps[0:TP, a_bank["s2", 2 * i + half], 0:W2C],
                                               ACT.Exp, scale=DH ** -0.5).then_inc(q["s2_free"], 1)
                            if i >= 20 and i % 20 == 3:
                                gathered(i // 20 - 1)
                        yield ATT
                        gathered(NG - 1)
                        for i, name in enumerate(("AT", "AT4")):
                            yield ATT + TT + i
                            turned(name, aTb)

                    run(pass_a, pass_b)

                @block.gpsimd
                def _(pool):
                    def inverse_root(i):
                        pool.wait_ge(q[f"var{i + 1}"], 1)
                        pool.tensor_tensor(rstd[:, i, :], var_e[:, i, :], neg_half[:, :],
                                           ALU.pow).then_inc(q[f"rstd{i + 1}"], 1)

                    def pass_a():
                        yield AT["ln1"]
                        inverse_root(0)
                        for i, pre in enumerate("qk"):
                            for g in range(2):
                                yield AT[f"{pre}{g}"]
                                pool.wait_ge(q["mid"], 2 * i + g + 1)
                                pool.tensor_tensor(part[i][:, 2, g, :], left[i][:, g, :], part[i][:, 1, g, :],
                                                   ALU.subtract).then_inc(q["lo"], 1)
                        yield AT["top"]
                        pool.wait_ge(q["top"], 1)
                        pool.partition_all_reduce(top_k[:, 1, :], top_k[:, 0, :], TP, RMAX).then_inc(q["top_all"], 1)
                        for t in range(TT):
                            yield AT[f"fk{t}"]
                            taken(pool, f"fk{t}")
                            pool.tensor_scalar(fk[:, t, :], fk[:, t, :], 1e-4, None, ALU.add).then_inc(q["eps_k"], 1)
                        for p in range(H // 2):
                            yield AT[f"fq{p}"]
                            taken(pool, f"fq{p}")
                            pool.tensor_scalar(fq[:, p, :], fq[:, p, :], 1e-4, None, ALU.add).then_inc(q["eps_q"], 1)
                        yield AT["wo4"]
                        inverse_root(1)
                        inverse_root(2)
                        yield AT["prob"]
                        pool.wait_ge(q["y"], TT)
                        pool.tensor_tensor(y[:, :, :], y[:, :, :],
                                           gamma_s[:, :].unsqueeze(1).to_broadcast([TP, TT, C]),
                                           ALU.mult).then_inc(q["gamma"], 1)
                        pool.wait_ge(q["gamma"], 1)
                        pool.tensor_tensor(y[:, :, :], y[:, :, :],
                                           beta_s[:, :].unsqueeze(1).to_broadcast([TP, TT, C]),
                                           ALU.add).then_inc(q["beta"], 1)

                    def pass_b():
                        yield 0
                        pool.tensor_copy(gate_b[:, :, :], gate[:, :, :]).then_inc(q["kept"], 1)
                        pool.tensor_tensor(base_b[:, :, :], h1[:, :, :], u[:, :, :], ALU.add).then_inc(q["kept"], 1)
                        for i in range(2):
                            for g in range(2):
                                yield 2 + 2 * i + g
                                pool.wait_ge(q["mid_b"], 2 * i + g + 1)
                                pool.tensor_tensor(part_b[:, 2, g, :], left_b[:, g, :], part_b[:, 1, g, :],
                                                   ALU.subtract).then_inc(q["lo_b"], 1)

                    run(pass_a, pass_b)

                @block.vector
                def _(dve):
                    n = 0

                    def go(ins):
                        nonlocal n
                        n += 1
                        ins.then_inc(q["chain"], 1)

                    def settle():
                        dve.wait_ge(q["chain"], n)

                    def link(ins):
                        go(ins)
                        settle()

                    unread_by = []

                    def place():
                        if len(unread_by) >= UNREAD:
                            dve.wait_ge(q["chain"], unread_by[-UNREAD])
                        unread_by.append(n + 1)
                        return unread[:, len(unread_by) % UNREAD, :]

                    def statistics(src, i, eps, signal, slot, gap):
                        for t in range(TT):
                            yield slot + gap * t
                            go(dve.bn_stats(st[:, i, t, :], src[:, t, :]))
                        yield slot + gap * TT
                        settle()
                        for t in range(TT):
                            go(dve.bn_aggr(mv[:, i, t, :], st[:, i, t, :]))
                        settle()
                        dve.tensor_scalar(var_e[:, i, :], mv[:, i, :, 1], eps, None, ALU.add).then_inc(q[signal], 1)

                    def normalized(dst, src, i, signal, slot, gap):
                        for t in range(TT):
                            yield slot + gap * t
                            if t == 0:
                                dve.wait_ge(q[f"rstd{i + 1}"], 1)
                            dve.tensor_scalar(dst[:, t, :], src[:, t, :], mv[:, i, t, 0:1], rstd[:, i, t:t + 1],
                                              ALU.subtract, ALU.mult).then_inc(q[signal], 1)

                    def divided(name, i, t, dst):
                        filled(dve, name)
                        v = ps[0:TP, bank(name), 0:NG * 128].rearrange("p (h c) -> p h c", c=2 * DH)
                        link(dve.reciprocal(den[:, i, t, :], v[:, :, DH]))
                        takes(dve.tensor_tensor(dst[:, t, :].rearrange("p (h d) -> p h d", d=DH), v[:, :, 0:DH],
                                                den[:, i, t, :].unsqueeze(2).to_broadcast([TP, H, DH]), ALU.mult),
                              name)

                    def pass_a():
                        yield AT["ln1"]
                        dve.wait_ge(q["tok_in"], 16)
                        yield from statistics(tok, 0, 1e-5, "var1", AT["ln1"], 0)
                        yield from normalized(xn, tok, 0, "xn", AT["xn"], 0)
                        for i, pre in enumerate("qk"):
                            for g in range(2):
                                name = f"{pre}{g}"
                                yield AT[name]
                                dve.wait_ge(q["sq"], 2 * i + g + 1)
                                takes(dve.tensor_tensor(split2(left[i][:, g, :]), halves(name),
                                                        split2(part[i][:, 0, g, :]), ALU.subtract), name)
                        for i, pre in enumerate(("mq", "mk")):
                            for t in range(TT):
                                yield AT[f"{pre}{t}"]
                                filled(dve, f"{pre}{t}")
                                takes(dve.tensor_reduce(top[:, i, t, :],
                                                        wide(f"{pre}{t}").rearrange("p (h m) -> p h m", m=M), AX.X,
                                                        ALU.max), f"{pre}{t}")
                        yield AT["top"]
                        taken(dve, f"mk{TT - 1}")
                        dve.tensor_reduce(top_k[:, 0, :], top[:, 1, :, :].rearrange("p t h -> p h t"), AX.X,
                                          ALU.max).then_inc(q["top"], 1)
                        go(dve.scalar_tensor_tensor(out=shift[:, 0, :, :], in0=squares[:, 0, :, :], scalar=-0.25,
                                                    in1=top[:, 0, :, :], op0=ALU.mult, op1=ALU.subtract))
                        yield AT["shift"]
                        dve.wait_ge(q["top_all"], 1)
                        link(dve.scalar_tensor_tensor(
                            out=shift[:, 1, :, :], in0=squares[:, 1, :, :], scalar=-0.25,
                            in1=top_k[:, 1, :].unsqueeze(1).to_broadcast([TP, TT, H]),
                            op0=ALU.mult, op1=ALU.subtract))
                        p = [sh_p[:, :, :, k, :].rearrange("p t i h -> p i t h") for k in range(NPART)]
                        for i in range(2):
                            go(dve.tensor_copy(p[0][:, i], shift[:, i, :, :]))
                        settle()
                        link(dve.tensor_tensor(sh_l[:, :, :, :], shift[:, :, :, :], p[0], ALU.subtract))
                        link(dve.tensor_copy(p[1], sh_l[:, :, :, :]))
                        dve.tensor_tensor(p[2], sh_l[:, :, :, :], p[1], ALU.subtract).then_inc(q["shift_parts"], 1)
                        yield AT["ctxT"]
                        filled(dve, "ctxT")
                        src = ps[:, bank("ctxT"), 0:NG * 128].rearrange("p (g j c) -> p g j c", j=2, c=2 * DH)
                        dst = ctx_d[:, :, :].rearrange("p g c -> p (g c)").rearrange("p (g j c) -> p g j c", j=2,
                                                                                     c=2 * DH)
                        dve.tensor_copy(dst[0:M, :, 0, :], src[0:M, :, 0, :])
                        takes(dve.tensor_copy(dst[M:, :, 1, :], src[M:, :, 1, :]), "ctxT")
                        for t in range(TT):
                            yield AT[f"ndT{t}"]
                            divided(f"ndT{t}", 0, t, at)
                        for t in range(TT):
                            name = "wo" if t < TT - 1 else "wo4"
                            if t in (0, TT - 1):
                                yield AT[name]
                            filled(dve, name)
                            ins = dve.tensor_tensor(h1[:, t, :], tok[:, t, :], tile_of("wo", "wo4", t), ALU.add)
                            if t >= TT - 2:
                                takes(ins, name)
                        yield AT["ln2"]
                        taken_all(dve, ["wo", "wo4"])
                        yield from statistics(h1, 1, 1e-5, "var2", AT["ln2"], SPREAD["norm"])
                        yield from normalized(u, h1, 1, "u", AT["u"], SPREAD["norm"])
                        yield AT["ln3"]
                        dve.wait_ge(q["u"], TT)
                        yield from statistics(u, 2, 1e-6, "var3", AT["ln3"], SPREAD["norm"])
                        for t in range(TT):
                            for e in range(E):
                                yield AT["router"] + SPREAD["router"] * (t + e / E)
                                go(dve.tensor_tensor_reduce(place()[:, 0:C], u[:, t, :], wr_s[:, e, :], 1.0, 0.0,
                                                              ALU.mult, ALU.add, lg[:, t, e:e + 1]))
                        yield AT["prob"]
                        settle()
                        link(dve.tensor_reduce(lg_s[:, 0, :], lg[:, :, :], AX.X, ALU.max))
                        dve.tensor_tensor(pr[:, 1, :, :], lg[:, :, :],
                                          lg_s[:, 0, :].unsqueeze(2).to_broadcast([TP, TT, E]),
                                          ALU.subtract).then_inc(q["logits"], 1)
                        yield from normalized(y, u, 2, "y", AT["y"], SPREAD["norm"])
                        yield AT["exps"]
                        dve.wait_ge(q["exps"], 1)
                        link(dve.tensor_reduce(lg_s[:, 1, :], pr[:, 0, :, :], AX.X, ALU.add))
                        link(dve.reciprocal(lg_s[:, 2, :], lg_s[:, 1, :]))
                        dve.tensor_tensor(pr[:, 2, :, :], pr[:, 0, :, :],
                                          lg_s[:, 2, :].unsqueeze(2).to_broadcast([TP, TT, E]),
                                          ALU.mult).then_inc(q["prob"], 1)
                        for t in range(TT):
                            for e in range(E):
                                yield AT["ranks"] + SPREAD["ranks"] * (t + e / E)
                                if t == e == 0:
                                    dve.wait_ge(q["prob"], 1)
                                    dve.wait_ge(q["prob_in"], 16)
                                go(dve.scalar_tensor_tensor(out=place().bitcast(BF16)[:, 0:K], in0=prow[:, :, e],
                                                              scalar=pr[:, 2, t, e:e + 1], in1=tie[:, t, :],
                                                              op0=ALU.subtract, op1=ALU.is_gt,
                                                              accum_out=rank2[:, t, e:e + 1]))
                        yield AT["ym"]
                        settle()
                        link(dve.tensor_scalar(chosen[:, :, :], rank2[:, :, :].rearrange("p t e -> p e t"),
                                               float(CAP), None, ALU.is_lt))
                        link(dve.tensor_tensor(gate[:, :, :], chosen[:, :, :],
                                               pr[:, 2, :, :].rearrange("p t e -> p e t"), ALU.mult))
                        for e in range(E - 2, -1, -1):
                            go(dve.tensor_tensor(chosen[:, e, :], chosen[:, e, :], chosen[:, e + 1, :], ALU.add))
                            link(dve.tensor_tensor(gate[:, e, :], gate[:, e, :], gate[:, e + 1, :], ALU.add))
                        if with_b:
                            filled(dve, "yT4")
                        dve.wait_ge(q["beta"], 1)
                        for e, (lo, hi) in enumerate(BANDS):
                            go(dve.tensor_tensor(ym[:, :, lo:hi], y[:, :, lo:hi],
                                                 chosen[:, e, :].unsqueeze(2).to_broadcast([TP, TT, hi - lo]),
                                                 ALU.mult))
                        link(dve.tensor_copy(ym[:, :, C:], chosen[:, 0, :].unsqueeze(2)))

                    item = 0

                    def maxima(g):
                        dve.wait_ge(q["s1_free"], item)
                        r0, r1 = neg[:, 0, :, :], neg[:, 1, :, :]
                        p = [neg_p[:, g, :, k, :] for k in range(NPART)]
                        link(dve.tensor_reduce(r0, mxh[:, GH * g:GH * (g + 1), :, :].rearrange("p h t a -> p t h a"),
                                               AX.X, ALU.max, negate=True))
                        link(dve.tensor_copy(p[0], r0))
                        link(dve.tensor_tensor(r1, r0, p[0], ALU.subtract))
                        link(dve.tensor_copy(p[1], r1))
                        dve.tensor_tensor(p[2], r1, p[1], ALU.subtract).then_inc(q["neg_parts"], 1)
                        dve.wait_ge(q["neg_parts"], g + 1)

                    def pass_b():
                        nonlocal item
                        yield 0
                        dve.memset(yT[:, :, K:], 0.0).then_inc(q["ones"], 1)
                        for i, pre in enumerate("QK"):
                            for g in range(2):
                                name = f"{pre}{g}"
                                yield 2 + 2 * i + g
                                dve.wait_ge(q["hi_b"], 2 * i + g + 1)
                                takes(dve.tensor_tensor(split2(left_b[:, g, :]), halves(name),
                                                        split2(part_b[:, 0, g, :]), ALU.subtract), name)
                        for step in range(ROWS_AT[-1] + 1):
                            yield PRE + step
                            if step < NS:
                                h, t = GH * (step // 20) + step % GH, step % 20 // GH
                                for half in range(2):
                                    dve.wait_ge(q["s1_ready"], item + 1)
                                    dve.tensor_reduce(mxh[:, h, t, half:half + 1],
                                                      ps[0:TP, a_bank["s1", item], 0:W2C - half],
                                                      AX.X, ALU.max).then_inc(q["s1_free"], 1)
                                    item += 1
                            if step % 20 == 19 and step < NS:
                                maxima(step // 20)
                            if step in ROWS_AT:
                                g = ROWS_AT.index(step)
                                dve.wait_ge(q["s1_ready"], item + 1)
                                dve.tensor_copy(
                                    rows[:, g, 0:K].rearrange("p (t c) -> p t c", t=TT),
                                    ps[0:NPART * GH, a_bank["s1", item], :].bitcast(BF16)[:, 0:106 * TT].rearrange(
                                        "p (t c) -> p t c", t=TT)[:, :, 0:TP]).then_inc(q["s1_free"], 1)
                                item += 1
                        for t in range(TT):
                            yield ATT + t
                            divided(f"NdT{t}", 1, t, atb)
                        dve.wait_ge(q["kept"], 2)
                        for t in range(TT):
                            yield ATT + TT + 2 + t
                            filled(dve, f"z{t}")
                            takes(dve.tensor_tensor(z[:, t, :], ps[0:TP, bank(f"z{t}"), 0:C], b2_s[:, :], ALU.add),
                                  f"z{t}")
                            taken(dve, f"z{t}")
                            for e, (lo, hi) in enumerate(BANDS):
                                dve.scalar_tensor_tensor(out=z[:, t, lo:hi], in0=z[:, t, lo:hi],
                                                         scalar=gate_b[:, e, t:t + 1], in1=base_b[:, t, lo:hi],
                                                         op0=ALU.mult, op1=ALU.add).then_inc(q["res"], 1)

                    run(pass_a, pass_b)
            nc.all_engine_barrier(sems_to_clear=every)

        one_round(0, None, True, False)
        with nc.Fori(1, B) as b:
            one_round(b, b - 1, True, True)
        one_round(None, B - 1, False, True)


def kernel(x, L0_tok_w, L0_tok_b, L0_attn_Wq, L0_attn_Wk, L0_attn_Wv, L0_attn_Wo, L0_attn_proj, L0_ffn_w_router,
           L0_ffn_gamma1, L0_ffn_beta1, L0_ffn_w1, L0_ffn_b1, L0_ffn_w2, L0_ffn_b2):
    import numpy as np
    import concourse.bacc as bacc
    from concourse.bass_utils import run_bass_kernel_spmd

    nc = bacc.Bacc("TRN2", target_bir_lowering=False, num_devices=1)
    laid = {
        "x": x, "tok_w": np.asarray(L0_tok_w).reshape(1, C), "tok_b": np.asarray(L0_tok_b).reshape(1, 1),
        "wq": L0_attn_Wq, "wk": L0_attn_Wk, "wv": L0_attn_Wv, "wo": L0_attn_Wo,
        "projT": np.asarray(L0_attn_proj).T, "wr": L0_ffn_w_router,
        "gamma": np.asarray(L0_ffn_gamma1).reshape(1, C), "beta": np.asarray(L0_ffn_beta1).reshape(1, C),
        "w1T": np.asarray(L0_ffn_w1).T, "b1": np.asarray(L0_ffn_b1).reshape(1, FC1),
        "w2T": np.asarray(L0_ffn_w2).T, "b2": np.asarray(L0_ffn_b2).reshape(1, 2 * C),
    }
    arrays = {f"in_{name}": np.ascontiguousarray(a) for name, a in laid.items()}
    aps = [nc.dram_tensor(name, a.shape, mybir.dt.from_np(a.dtype), kind="ExternalInput").ap()
           for name, a in arrays.items()]
    out = nc.dram_tensor("out_0", (B, K, C), F32, kind="ExternalOutput").ap()
    tower(nc, *aps, out)
    r = run_bass_kernel_spmd(nc, [arrays], core_ids=[0])
    return r.results[0]["out_0"]
```

```python
from contextlib import ExitStack

import concourse.bass as bass
from concourse import mybir

F32 = mybir.dt.float32
BF16 = mybir.dt.bfloat16
U32 = mybir.dt.uint32
ALU = mybir.AluOpType
ACT = mybir.ActivationFunctionType
AX = mybir.AxisListType
RMAX = bass.bass_isa.ReduceOp.max

B, N, C = 8, 750, 192
SP_P, SP_T = 125, 6
K = int(round(N * 0.7))
TP, TT = 105, 5
W2C = 263
KP = 2 * W2C
H, DH, M = 12, 16, 64
CH = 96
NPART = 3
PART_A = (0, 0, 0, 1, 1, 1, 2)
PART_B = (0, 1, 2, 0, 1, 2, 0)
BLOCKS = len(PART_A)
SK = BLOCKS * DH
ONES_FROM = 96
E = 4
CAP = int(0.5 * K)
LOADS = 12 + E
SCORES_LEAD = 3
LOADS_FROM = 3
LOADS_EACH = -(-LOADS // (B - LOADS_FROM))
HID = 4 * C
FC1 = HID + 3 * C
BANDS = ((0, 24), (24, 48), (48, 96), (96, 192))
TINY = -(2.0 ** -126)
GH = 4
NG = H // GH
UNREAD = 2


FIRST_A = ["xT", "xT4", "q0", "q1", "k0", "k1", "v", "v4"]
NEXT_A = (
    ["ssT", "ss"] + [f"mq{t}" for t in range(TT)] + [f"mk{t}" for t in range(TT)] + ["shift"]
    + [f"fk{t}" for t in range(TT)] + [f"fq{p}" for p in range(H // 2)] + ["ctx", "ctxT"]
    + [f"nd{g}" for g in range(NG)] + [f"ndT{t}" for t in range(TT)] + ["aT", "aT4", "wo", "wo4"]
)
EARLY_B = ["yT", "yT4", "Q0", "Q1", "K0", "K1", "V", "V4"]
HIDDEN = [f"g{f}" for f in range(HID // 128)]
HIDDEN_PAIR = (2, 0, 1, 2, 1, 1)
LATE_B = [f"NdT{t}" for t in range(TT)] + ["AT", "AT4"] + [f"z{t}" for t in range(TT)]
GUESTS = [f"mk{t}" for t in range(0, TT, 2)]
FIRST_BANK = (0, 2, 4, 6, 4)


def plan(with_a, with_b):
    order = []
    if with_a:
        order += [((i + 3) % 4, name) for i, name in enumerate(FIRST_A)]
        order += [(4 if name in GUESTS else 3, name) for name in NEXT_A]
    if with_b:
        order += [(i % 3, name) for i, name in enumerate(EARLY_B)] + list(zip(HIDDEN_PAIR, HIDDEN))
        order += [(i % 3, name) for i, name in enumerate(LATE_B)]
    count, jobs = [0] * len(FIRST_BANK), {}
    for pair, name in order:
        count[pair] += 1
        jobs[name] = pair, count[pair]
    return jobs


PV_BANK = 4
NS = 20 * NG
OFF = 29
PV_LAG = 3
ROWS_AT = (22, 46, 63)
RANKS_AT, EARLY = 0, 6
LEFT_AT = 2.75
PRE = EARLY + len(EARLY_B) + 4
HIDDEN_AT = {name: PRE + (-4, -3, -2, -1, 2, 5)[i] for i, name in enumerate(HIDDEN)}
HIDDEN_END = 7
ATT = PRE + NS + OFF + PV_LAG + 1


AT = {"ln1": 115, "xn": 118, "xT": 0.5, "xT4": 0.6, "q0": 1, "q1": 2, "k0": 2, "k1": 2, "v": 2, "v4": 2.5, "ss": 7,
      "top": 24, "shift": 28, "ctx": 67, "ctxT": 69, "aT": 77, "aT4": 77.8, "wo": 78.6, "wo4": 82.56, "ln2": 82.56,
      "u": 87.06, "ln3": 87.06, "router": 93.86, "prob": 99.26, "y": 99.36, "exps": 99.36, "mq0": 12, "mq1": 13,
      "mq2": 14, "mq3": 16, "mq4": 17, "mk0": 21, "mk1": 22, "mk2": 23, "mk3": 23, "mk4": 24, "fk0": 34, "fk1": 36.5,
      "fk2": 40, "fk3": 41.65, "fk4": 43.3, "fq0": 45.5, "fq1": 47.15, "fq2": 48.8, "fq3": 50.45, "fq4": 52.1,
      "fq5": 52.1, "nd0": 70, "nd1": 71, "nd2": 72, "ndT0": 73, "ndT1": 73.8, "ndT2": 74.6, "ndT3": 75.4,
      "ndT4": 76.2, "load": 84}
SPREAD = {"norm": 0.5, "router": 1.5, "ranks": 1}


def attention_banks():
    bank, before, held, count = {}, {}, {}, {"s1": 0, "s2": 0}

    def item(kind, ring):
        key = (kind, count[kind])
        b = min(ring, key=lambda r: held.get(r, (-1, None))[0])
        bank[key], before[key] = b, held.get(b, (-1, None))[1]
        held[b] = (sum(count.values()), key)
        count[kind] += 1

    for step in range(NS + OFF):
        for _ in range(2 * (step < NS) + (step in ROWS_AT)):
            item("s1", range(4) if HIDDEN_END <= step < OFF - 2 else range(2))
        if step >= OFF:
            for _ in range(2):
                item("s2", range(4) if step > ROWS_AT[-1] else range(2, 4))
    return bank, before


def weave(*programs):
    due = [next(p, None) for p in programs]
    while any(d is not None for d in due):
        i = min((d, i) for i, d in enumerate(due) if d is not None)[1]
        due[i] = next(programs[i], None)


def rows_item(g):
    return 2 * min(ROWS_AT[g] + 1, NS) + g


def tower(nc, x, tok_w, tok_b, wq, wk, wv, wo, projT, wr, gamma, beta, w1T, b1, w2T, b2, out):
    ctx = ExitStack()
    with ctx:
        def sb(name, shape, dt=F32):
            return ctx.enter_context(nc.sbuf_tensor(name, shape, dt))

        def sem(name):
            return ctx.enter_context(nc.semaphore(name))

        ps = ctx.enter_context(nc.psum_tensor("ps", [128, 8, 512], F32))
        sorted_x = nc.dram_tensor("sorted_x", [B * N, C], F32).ap()
        score_row = nc.dram_tensor("score_row", [B, 1, N], F32).ap()
        prob_row = nc.dram_tensor("prob_row", [1, K * E], F32).ap()
        part_d = [nc.dram_tensor(f"part_d{i}", [NPART, C, KP], BF16).ap() for i in range(4)]

        ident = sb("ident", [128, 128])
        ident_b = sb("ident_b", [128, 128], BF16)
        head_of = sb("head_of", [CH, 2, 2 * DH])
        neg_half = sb("neg_half", [TP, TT])
        wq_s, wk_s, wv_s, wo_s = (sb(f"w{n}_s", [CH, 2, C]) for n in "qkvo")
        w1_s = sb("w1_s", [CH + 1, 2, FC1])
        w2h_s = sb("w2h_s", [128, HID // 128, C])
        w2a_s = sb("w2a_s", [CH, 2, C])
        b2_s = sb("b2_s", [TP, C])
        gamma_s = sb("gamma_s", [TP, C])
        beta_s = sb("beta_s", [TP, C])
        wr_s = sb("wr_s", [TP, E, C])
        pj = sb("pj", [DH, M])
        pj_r = sb("pj_r", [DH, 2, M])
        pj_b = sb("pj_b", [DH, NPART, M], BF16)
        proj_k = sb("proj_k", [SK + NPART, M], BF16)
        tie = sb("tie", [TP, TT, K], BF16)

        s = {}
        for name in ("setup", "ones", "w_in", "tok_w_in", "pj_out", "chain_p", "chain_v", "x_in0", "x_in1", "product",
                     "score", "score_out", "row_in0", "row_in1", "rank", "tie", "target"):
            s[name] = sem("s_" + name)
        once = [s[n] for n in s]
        scattered = sem("scattered")

        with ExitStack() as inner:
            def sbi(name, shape, dt=F32):
                return inner.enter_context(nc.sbuf_tensor(name, shape, dt))

            xs = sbi("xs", [SP_P, B, SP_T, C])
            tw = sbi("tw", [SP_P, C])
            tb = sbi("tb", [SP_P, 1])
            prod = sbi("prod", [SP_P, SP_T, C])
            score = sbi("score", [SP_P, B, SP_T])
            score_b = sbi("score_b", [SP_P, B, SP_T])
            row = sbi("row", [SP_P, B, N])
            above = sbi("above", [SP_P, SP_T, N], BF16)
            rank = sbi("rank", [SP_P, B, SP_T])
            base = sbi("base", [SP_P, B, SP_T])
            target = sbi("target", [SP_P, B, SP_T], U32)
            tie_s = sbi("tie_s", [SP_P, SP_T, N], BF16)
            w2h_in = sbi("w2h_in", [128, HID // 128, 2 * C])
            w2a_in = sbi("w2a_in", [CH, 2, 2 * C])
            b2_in = sbi("b2_in", [TP, 2 * C])
            with nc.Block() as block:
                @block.scalar
                def _(act):
                    act.dma_start(tw[:, :], tok_w.to_broadcast([SP_P, C])).then_inc(s["tok_w_in"], 16)
                    act.dma_start(tb[:, :], tok_b.to_broadcast([SP_P, 1])).then_inc(s["tok_w_in"], 16)

                    for b in range(B):
                        if b >= 2:
                            act.wait_ge(s[f"x_in{b % 2}"], 16 * (b // 2))
                        act.dma_start(xs[:, b, :, :],
                                      x[b].rearrange("(p t) d -> p t d", t=SP_T)).then_inc(s[f"x_in{b % 2}"], 16)

                @block.sync
                def _(sp):
                    loads = [(pj[:, :], projT)]
                    for dst, src in ((wq_s, wq), (wk_s, wk), (wv_s, wv), (wo_s, wo)):
                        loads.append((dst[:, :, :], src.rearrange("(k p) n -> p k n", k=2)))
                    loads += [
                        (w1_s[0:CH, :, :], w1T.rearrange("(k p) n -> p k n", k=2)),
                        (w1_s[CH:CH + 1, 1, :], b1),
                        (w2h_in[:, :, :], w2T[0:HID, :].rearrange("(k p) n -> p k n", p=128)),
                        (w2a_in[:, :, :], w2T[HID:, :].rearrange("(k p) n -> p k n", k=2)),
                        (b2_in[:, :], b2.to_broadcast([TP, 2 * C])),
                        (gamma_s[:, :], gamma.to_broadcast([TP, C])),
                        (beta_s[:, :], beta.to_broadcast([TP, C])),
                    ]
                    loads += [(wr_s[:, e, :], wr[e:e + 1, :].to_broadcast([TP, C])) for e in range(E)]
                    for b in range(B):
                        sp.wait_ge(s["score"], b + 1)
                        sp.dma_start(score_row[b].rearrange("a (p t) -> (a p) t", t=SP_T),
                                     score_b[:, b, :]).then_inc(s["score_out"], 16)
                        sp.wait_ge(s["score_out"], 16 * (b + 1))
                        if b >= 2:
                            sp.wait_ge(s[f"row_in{b % 2}"], 16 * (b // 2))
                        sp.dma_start(row[:, b, :], score_row[b].to_broadcast([SP_P, N])).then_inc(
                            s[f"row_in{b % 2}"], 16)
                        if b >= LOADS_FROM:
                            for dst, src in loads[LOADS_EACH * (b - LOADS_FROM):LOADS_EACH * (b - LOADS_FROM + 1)]:
                                sp.dma_start(dst, src).then_inc(s["w_in"], 16)
                    sp.wait_ge(s["ones"], 1)
                    sp.wait_ge(s["setup"], 1)
                    for i, part in enumerate(PART_B):
                        sp.dma_start(proj_k[DH * i:DH * (i + 1), :], pj_b[:, part, :]).then_inc(s["pj_out"], 16)
                    sp.wait_ge(s["pj_out"], 16 * len(PART_B))
                    sp.wait_ge(s["w_in"], 16 * LOADS)

                @block.vector
                def _(dve):
                    dve.wait_ge(s["tok_w_in"], 32)

                    def scores(b):
                        dve.wait_ge(s[f"x_in{b % 2}"], 16 * (b // 2 + 1))
                        for t in range(SP_T):
                            if b:
                                dve.wait_ge(s["product"], (b - 1) * SP_T + t + 1)
                            dve.tensor_tensor_reduce(prod[:, t, :], xs[:, b, t, :], tw[:, :], 1.0, 0.0,
                                                     ALU.mult, ALU.add, score[:, b, t:t + 1]).then_inc(s["product"], 1)
                        dve.wait_ge(s["product"], (b + 1) * SP_T)
                        dve.tensor_scalar(score_b[:, b, :], score[:, b, :], tb[:, 0:1], None,
                                          ALU.add).then_inc(s["score"], 1)

                    def ranks(b):
                        if b == 0:
                            dve.wait_ge(s["tie"], 2 + B)
                        dve.wait_ge(s["score"], b + 1)
                        dve.wait_ge(s[f"row_in{b % 2}"], 16 * (b // 2 + 1))
                        for t in range(SP_T):
                            if b:
                                dve.wait_ge(s["rank"], (b - 1) * SP_T + t + 1)
                            dve.scalar_tensor_tensor(out=above[:, t, :], in0=row[:, b, :],
                                                     scalar=score_b[:, b, t:t + 1], in1=tie_s[:, t, :],
                                                     op0=ALU.subtract, op1=ALU.is_gt,
                                                     accum_out=rank[:, b, t:t + 1]).then_inc(s["rank"], 1)
                        dve.wait_ge(s["rank"], (b + 1) * SP_T)
                        dve.tensor_tensor(target[:, b, :], rank[:, b, :], base[:, b, :],
                                          ALU.add).then_inc(s["target"], 1)

                    for b in range(B + SCORES_LEAD):
                        if b < B:
                            scores(b)
                        if b >= SCORES_LEAD:
                            ranks(b - SCORES_LEAD)
                    n = 0

                    def link(ins):
                        nonlocal n
                        n += 1
                        ins.then_inc(s["chain_v"], 1)
                        dve.wait_ge(s["chain_v"], n)

                    dve.memset(proj_k[ONES_FROM:, :], 1.0).then_inc(s["ones"], 1)
                    dve.wait_ge(s["w_in"], 16 * LOADS)
                    link(dve.tensor_copy(pj_b[:, 0, :], pj[:, :]))
                    link(dve.tensor_tensor(pj_r[:, 0, :], pj[:, :], pj_b[:, 0, :], ALU.subtract))
                    link(dve.tensor_copy(pj_b[:, 1, :], pj_r[:, 0, :]))
                    dve.tensor_tensor(pj_b[:, 2, :], pj_r[:, 0, :], pj_b[:, 1, :], ALU.subtract).then_inc(s["setup"], 1)
                    link(dve.tensor_tensor(w2h_s[:, :, :], w2h_in[:, :, 0:C], w2h_in[:, :, C:], ALU.add))
                    link(dve.tensor_tensor(w2a_s[:, :, :], w2a_in[:, :, 0:C], w2a_in[:, :, C:], ALU.add))
                    link(dve.tensor_tensor(b2_s[:, :], b2_in[:, 0:C], b2_in[:, C:], ALU.add))

                @block.gpsimd
                def _(pool):
                    pool.memset(tie_s[:, :, :], TINY).then_inc(s["tie"], 1)
                    pool.wait_ge(s["tie"], 1)
                    pool.affine_select(out=tie_s[:, :, :], in_=tie_s[:, :, :], compare_op=ALU.is_gt, fill=0.0,
                                       base=0, pattern=[[1, SP_T], [-1, N]],
                                       channel_multiplier=SP_T).then_inc(s["tie"], 1)
                    for i in range(B):
                        pool.memset(base[:, i, :], float(N * i)).then_inc(s["tie"], 1)
                    n = 0

                    def link(ins):
                        nonlocal n
                        n += 1
                        ins.then_inc(s["chain_p"], 1)
                        pool.wait_ge(s["chain_p"], n)

                    link(pool.memset(ident[:, :], 0.0))
                    link(pool.affine_select(out=ident[:, :], in_=ident[:, :], compare_op=ALU.not_equal, fill=1.0,
                                            base=0, pattern=[[-1, 128]], channel_multiplier=1))
                    link(pool.tensor_copy(ident_b[:, :], ident[:, :]))
                    link(pool.memset(head_of[:, :, :], 1.0))
                    link(pool.affine_select(out=head_of[:, :, :], in_=head_of[:, :, :], compare_op=ALU.is_ge, fill=0.0,
                                            base=0, pattern=[[CH, 2], [-DH, 2 * DH]], channel_multiplier=1))
                    link(pool.affine_select(out=head_of[:, :, :], in_=head_of[:, :, :], compare_op=ALU.is_ge, fill=0.0,
                                            base=DH - 1, pattern=[[-CH, 2], [DH, 2 * DH]], channel_multiplier=-1))
                    link(pool.memset(neg_half[:, :], -0.5))
                    link(pool.memset(tie[:, :, :], TINY))
                    link(pool.affine_select(out=tie[:, :, :], in_=tie[:, :, :], compare_op=ALU.is_gt, fill=0.0,
                                            base=0, pattern=[[1, TT], [-1, K]], channel_multiplier=TT))
                    for b in range(B):
                        pool.wait_ge(s["target"], b + 1)
                        for t in range(SP_T):
                            pool.indirect_dma_start(sorted_x,
                                                    bass.IndirectOffsetOnAxis(ap=target[:, b, t:t + 1], axis=0),
                                                    xs[:, b, t, :], None).then_inc(scattered, 16)
                    pool.wait_ge(scattered, 16 * SP_T * B)
            nc.all_engine_barrier(sems_to_clear=range(once[0].num, once[-1].num + 1))

        tok = sb("tok", [TP, TT, C])
        st = sb("st", [TP, 3, TT, 6])
        mv = sb("mv", [TP, 3, TT, 2])
        var_e = sb("var_e", [TP, 3, TT])
        rstd = sb("rstd", [TP, 3, TT])
        xn = sb("xn", [TP, TT, C])
        xT = sb("xT", [CH, 2, KP])
        work = sb("work", [128, 10 * KP])
        left = [work[0:CH, 2 * KP * i:2 * KP * (i + 1)].rearrange("p (g c) -> p g c", g=2) for i in range(2)]
        part = [work[0:CH, (4 + 3 * i) * KP:(7 + 3 * i) * KP].bitcast(BF16).rearrange(
            "p (k g c) -> p k g c", k=NPART, g=2) for i in range(2)]
        fq = work[:, 0:H // 2 * KP].rearrange("p (h c) -> p h c", c=KP)
        pq = sb("pq", [SK + NPART, H, KP], BF16)
        pk = sb("pk", [SK + NPART, H, KP], BF16)
        vp = sb("vp", [TP, TT, H, 2 * DH])
        squares = sb("squares", [TP, 2, TT, H])
        top = sb("top", [TP, 2, TT, H])
        top_k = sb("top_k", [TP, 2, H])
        shift = sb("shift", [TP, 2, TT, H])
        sh_l = sb("sh_l", [TP, 2, TT, H])
        sh_p = sb("sh_p", [TP, TT, 2, NPART, H], BF16)
        sh_row = sb("sh_row", [2 * NPART * H, KP], BF16)
        fk_nd = sb("fk_nd", [128, TT * H * M])
        prow = fk_nd[0:TP, 0:K * E].rearrange("p (k e) -> p k e", e=E)
        fk = fk_nd[0:TP, :].rearrange("p (t f) -> p t f", t=TT)
        nd = fk_nd[:, 0:NG * KP].rearrange("p (g c) -> p g c", g=NG)
        cT = sb("cT", [128, NG, 2 * M])
        ctx_d = sb("ctx_d", [128, NG, 128])
        den = sb("den", [TP, 2, TT, H])
        u = sb("u", [TP, TT, C])
        ym = sb("ym", [TP, TT, C + 1])
        lg = sb("lg", [TP, TT, E])
        lg_s = sb("lg_s", [TP, 4, TT])
        pr = sb("pr", [TP, 3, TT, E])
        unread = sb("unread", [TP, UNREAD, W2C])
        rank2 = sb("rank2", [TP, TT, E])
        chosen = sb("chosen", [TP, E, TT])
        gate = sb("gate", [TP, E, TT])
        h1, at, y, aT = tok, xn, ym[:, :, 0:C], xT

        yT_nd = sb("yT_nd", [128, NG, KP])
        yT = yT_nd[0:CH + 1, 0:2, :]
        ndb = yT_nd
        gT_w = sb("gT_w", [128, H // 2 * KP])
        gT = gT_w[:, :].rearrange("p (f c) -> p f c", c=KP)
        left_b = gT_w[0:CH, 0:2 * KP].rearrange("p (g c) -> p g c", g=2)
        sa = sb("sa", [SK + NPART, H, KP], BF16)
        sk = sb("sk", [SK + NPART, H, KP], BF16)
        va = sb("va", [TP, TT, H, 2 * DH])
        pT = sb("pT", [TP, 2, GH, KP])
        sq = pT[0:CH, 0, :, :].rearrange("p (i g) c -> p i g c", g=2)
        ssT = pT[0:64, 1, 3, :]
        part_b = [w.bitcast(BF16).rearrange("p (k g c) -> p k g c", k=NPART, g=2) for w in (
            gT_w[0:CH, 2 * KP:5 * KP], pT[0:CH, 1, 0:3, :].rearrange("p a c -> p (a c)"))]
        mxh = sb("mxh", [TP, H, TT, 2])
        neg = sb("neg", [TP, 2, TT, GH])
        neg_p = sb("neg_p", [TP, NG, TT, NPART, GH], BF16)
        rows = sb("rows", [NPART * GH, NG, KP], BF16)
        late = sa[0:TP, :, :].rearrange("p h c -> p (h c)").bitcast(F32)
        atb = late[:, 0:TT * C].rearrange("p (t c) -> p t c", t=TT)
        aTb = late[0:CH, TT * C:TT * C + 2 * KP].rearrange("p (g c) -> p g c", g=2)
        base_b = sb("base_b", [TP, TT, C])
        z = atb

        names = ("constant_v constant_p tok_in h_in var1 var2 var3 rstd1 rstd2 rstd3 xn sq mid lo stack_q "
                 "stack_k top top_all shift_parts shift_in eps_k eps_q u y gamma beta logits exps prob "
                 "prob_out prob_in ym chain kept hi_b mid_b lo_b stack_b ones neg_parts neg_in s1_ready "
                 "s1_free s2_ready s2_free p_used pv_free res stored").split()
        q = {n: sem("q_" + n) for n in names}
        away_sem = [[sem(f"q_away{i}{k}") for k in range(NPART)] for i in range(4)]
        split = part + part_b
        ready = [sem(f"q_ps_ready{i}") for i in range(len(FIRST_BANK))]
        free = [sem(f"q_ps_free{i}") for i in range(len(FIRST_BANK))]
        every = range(q[names[0]].num, free[-1].num + 1)

        jobs = {}

        def bank(name):
            return FIRST_BANK[jobs[name][0]]

        a_bank, a_before = attention_banks()

        def bank_free(pe, key):
            if key is not None:
                pe.wait_ge(q[key[0] + "_free"], key[1] + 1)

        def filled(eng, name):
            eng.wait_ge(ready[jobs[name][0]], jobs[name][1])

        def taken(eng, name):
            eng.wait_ge(free[jobs[name][0]], jobs[name][1])

        def taken_all(eng, some):
            for name in some:
                taken(eng, name)

        def takes(ins, name):
            ins.then_inc(free[jobs[name][0]], 1)

        def cols(t):
            return slice(t * TP, (t + 1) * TP)

        def halves(name, m=CH):
            return ps[0:m, bank(name):bank(name) + 2, 0:W2C]

        def wide(name):
            return ps[0:TP, bank(name):bank(name) + 2, :].rearrange("p a c -> p (a c)")[:, 0:H * M]

        def tile_of(name, name4, t):
            k = bank(name) if t < TT - 1 else bank(name4)
            return ps[0:TP, k + t // 2 % 2, C * (t % 2):C * (t % 2 + 1)]

        def split2(ap):
            return ap.rearrange("p (a c) -> p a c", a=2)

        def kept_tokens(b):
            return sorted_x.rearrange("(b n) d -> b n d", b=B)[b, 0:K, :].rearrange("(p t) d -> p t d", t=TT)

        def one_round(c, a, b, d=None, last=False):
            with_a, with_b, with_c = a is not None, b is not None, c is not None
            jobs.clear()
            jobs.update(plan(with_a, with_b))
            with nc.Block() as block:
                def run(pass_a, pass_b, pass_c=None, pass_h=None):
                    weave(*([pass_a()] if with_a else []), *([pass_b()] if with_b else []),
                          *([pass_h()] if with_b and pass_h else []), *([pass_c()] if with_c and pass_c else []))

                @block.sync
                def _(sp):
                    def store(b):
                        sp.dma_start(out[b].rearrange("(p t) d -> p t d", t=TT), atb[:, :, :]).then_inc(
                            q["stored"], 16)

                    def away(i, part, signal, count):
                        sp.wait_ge(q[signal], count)
                        src = split[i]
                        sp.dma_start(part_d[i][part].rearrange("(g p) c -> p g c", g=2),
                                     src[:, part, :, :]).then_inc(away_sem[i][part], 16)

                    def back(i, part):
                        sp.wait_ge(away_sem[i][part], 16)
                        dst, order = ((pq, PART_A), (pk, PART_A), (sa, PART_A), (sk, PART_B))[i]
                        for r, k in enumerate(order):
                            if k == part:
                                sp.dma_start(dst[DH * r:DH * (r + 1), :, :],
                                             part_d[i][part].rearrange("(h d) c -> d h c", d=DH)).then_inc(
                                    q[("stack_q", "stack_k", "stack_b", "stack_b")[i]], 16)

                    def pass_a():
                        yield 0
                        if with_b:
                            sp.wait_ge(q["kept"], 1)
                        sp.dma_start(tok[:, :, :], kept_tokens(a)).then_inc(q["h_in"], 16)
                        yield AT["k0"]
                        away(0, 0, "sq", 2)
                        away(0, 1, "mid", 2)
                        back(0, 0)
                        away(0, 2, "lo", 2)
                        yield AT["v"]
                        away(1, 0, "sq", 4)
                        back(0, 1)
                        away(1, 1, "mid", 4)
                        back(0, 2)
                        back(1, 0)
                        away(1, 2, "lo", 4)
                        back(1, 1)
                        back(1, 2)
                        yield AT["shift"]
                        taken(sp, "shift")
                        for i, dst in enumerate((pq, pk)):
                            for k in range(NPART):
                                r = (i * NPART + k) * H
                                sp.dma_start(dst[SK + k:SK + k + 1, :, :],
                                             sh_row[r:r + H, :]).then_inc(q["shift_in"], 16)
                        yield AT["prob"]
                        sp.wait_ge(q["prob"], 1)
                        sp.dma_start(prob_row.rearrange("a (p t) -> (a p) t", t=TT * E),
                                     pr[:, 2, :, :].rearrange("p t e -> p (t e)")).then_inc(q["prob_out"], 16)
                        sp.wait_ge(q["prob_out"], 16)
                        sp.dma_start(fk_nd[0:TP, 0:K * E], prob_row.to_broadcast([TP, K * E])).then_inc(
                            q["prob_in"], 16)
                        yield ATT + len(LATE_B)
                        sp.wait_ge(q["prob_in"], 16)

                    def pass_b():
                        if d is not None:
                            yield 0
                            store(d)
                        yield EARLY + 4
                        away(2, 0, "hi_b", 2)
                        away(2, 1, "mid_b", 2)
                        if d is not None:
                            sp.wait_ge(q["stored"], 16)
                        back(2, 0)
                        away(2, 2, "lo_b", 2)
                        yield EARLY + 6
                        away(3, 0, "hi_b", 4)
                        back(2, 1)
                        away(3, 1, "mid_b", 4)
                        back(2, 2)
                        back(3, 0)
                        away(3, 2, "lo_b", 4)
                        back(3, 1)
                        back(3, 2)
                        for g in range(NG):
                            yield PRE + ROWS_AT[g]
                            sp.wait_ge(q["s1_free"], rows_item(g) + 1)
                            for k in range(NPART):
                                sp.dma_start(sa[SK + k:SK + k + 1, GH * g:GH * (g + 1), :],
                                             rows[GH * k:GH * (k + 1), g, :]).then_inc(q["neg_in"], 16)
                        yield ATT + len(LATE_B)
                        sp.wait_ge(q["res"], TT * len(BANDS))
                        if last:
                            store(b)
                            sp.wait_ge(q["stored"], 32)

                    def pass_c():
                        yield AT["load"]
                        if with_a:
                            filled(sp, "aT4")
                        sp.dma_start(xn[:, :, :], kept_tokens(c)).then_inc(q["tok_in"], 16)

                    run(pass_a, pass_b, pass_c)

                @block.tensor
                def _(pe):
                    def begin(name):
                        r, n = jobs[name]
                        if n > 1:
                            pe.wait_ge(free[r], n - 1)
                        return bank(name)

                    def end(ins, name):
                        ins.then_inc(ready[jobs[name][0]], 1)

                    def turn(name, src, more=0):
                        k = begin(name)
                        for t in ([TT - 1] if name.endswith("4") else range(TT - 1)):
                            for g in range(2):
                                m = CH + (more if g else 0)
                                ins = pe.transpose(ps[0:m, k + g, cols(t % (TT - 1))], src[:, t, CH * g:CH * g + m],
                                                   ident[0:TP, 0:TP])
                        end(ins, name)

                    def project(name, w, c0, m, src, more=0):
                        k = begin(name)
                        for i in range(2):
                            for g in range(2):
                                kk = CH + (more if g else 0)
                                ins = pe.matmul(ps[0:m, k + i, 0:W2C], w[0:kk, g, c0:c0 + m],
                                                src[0:kk, g, W2C * i:W2C * (i + 1)], start=(g == 0), stop=(g == 1))
                        end(ins, name)

                    def project_rows(name, w, c0, src, more=0):
                        begin(name)
                        for t in ([TT - 1] if name.endswith("4") else range(TT - 1)):
                            for g in range(2):
                                kk = CH + (more if g else 0)
                                ins = pe.matmul(tile_of(name, name, t), src[0:kk, g, cols(t)], w[0:kk, g, c0:c0 + C],
                                                start=(g == 0), stop=(g == 1))
                        end(ins, name)

                    def turn_nd(name, t, src):
                        k = begin(name)
                        for g in range(NG):
                            ins = pe.transpose(ps[0:TP, k, 128 * g:128 * (g + 1)], src[:, g, cols(t)], ident[:, :])
                        end(ins, name)

                    def features(name, src, depth, t):
                        k = begin(name)
                        for h in range(H):
                            ins = pe.matmul(ps[0:TP, k + h // 8, M * (h % 8):M * (h % 8 + 1)],
                                            src[0:depth, h, cols(t)], proj_k[0:depth, :], start=True, stop=True)
                        end(ins, name)

                    def pass_a():
                        yield AT["xT"]
                        turn("xT", xn)
                        yield AT["xT4"]
                        turn("xT4", xn)
                        taken_all(pe, ["xT", "xT4"])
                        for pre, w in (("q", wq_s), ("k", wk_s)):
                            for g in range(2):
                                yield AT[f"{pre}{g}"]
                                project(f"{pre}{g}", w, CH * g, CH, xT)
                        for name in ("v", "v4"):
                            yield AT[name]
                            project_rows(name, wv_s, 0, xT)
                        yield AT["ss"] - 1
                        k = begin("ssT")
                        pe.wait_ge(q["sq"], 4)
                        for half in range(2):
                            for g in range(2):
                                for i in range(2):
                                    ins = pe.matmul(ps[32 * i:32 * (i + 1), k + half, 0:W2C], head_of[:, g, :],
                                                    sq[:, i, g, W2C * half:W2C * (half + 1)],
                                                    start=(g == 0), stop=(g == 1))
                        end(ins, "ssT")
                        yield AT["ss"]
                        k = begin("ss")
                        taken(pe, "ssT")
                        for t in range(TT):
                            ins = pe.transpose(ps[0:TP, k, 64 * t:64 * (t + 1)], ssT[:, cols(t)], ident[0:64, 0:64])
                        end(ins, "ss")
                        for i, (src, pre) in enumerate(((pq, "mq"), (pk, "mk"))):
                            for t in range(TT):
                                yield AT[f"{pre}{t}"]
                                if f"{pre}{t}" == GUESTS[0] and with_b:
                                    taken(pe, "g3")
                                if t == 0:
                                    pe.wait_ge(q[("stack_q", "stack_k")[i]], 16 * BLOCKS)
                                features(f"{pre}{t}", src, SK, t)
                        yield AT["shift"]
                        k = begin("shift")
                        pe.wait_ge(q["shift_parts"], 1)
                        for t in range(TT):
                            ins = pe.transpose(ps[0:2 * NPART * H, k, :].bitcast(BF16)[:, 106 * t:106 * t + TP],
                                               sh_p[:, t, :, :, :].rearrange("p i k h -> p (i k h)"),
                                               ident_b[0:TP, 0:TP])
                        end(ins, "shift")
                        for t in range(TT):
                            yield AT[f"fk{t}"]
                            if t == 0:
                                pe.wait_ge(q["shift_in"], 16 * 2 * NPART)
                            features(f"fk{t}", pk, SK + NPART, t)
                        for p in range(H // 2):
                            yield AT[f"fq{p}"]
                            k = begin(f"fq{p}")
                            for i in range(2):
                                for j in range(2):
                                    ins = pe.matmul(ps[M * j:M * (j + 1), k + i, 0:W2C], proj_k[:, :],
                                                    pq[:, 2 * p + j, W2C * i:W2C * (i + 1)], start=True, stop=True)
                            end(ins, f"fq{p}")
                        yield AT["ctx"]
                        k = begin("ctx")
                        taken(pe, "v4")
                        pe.wait_ge(q["eps_k"], TT)
                        for g in range(NG):
                            for t in range(TT):
                                for j in range(GH):
                                    h = GH * g + j
                                    ins = pe.matmul(ps[32 * j:32 * (j + 1), k, M * g:M * (g + 1)],
                                                    vp[:, t, h, :], fk[:, t, M * h:M * (h + 1)],
                                                    start=(t == 0), stop=(t == TT - 1))
                        end(ins, "ctx")
                        yield AT["ctxT"]
                        k = begin("ctxT")
                        taken(pe, "ctx")
                        for g in range(NG):
                            ins = pe.transpose(ps[:, k, 128 * g:128 * (g + 1)], cT[:, g, :], ident[:, :])
                        end(ins, "ctxT")
                        for g in range(NG):
                            yield AT[f"nd{g}"]
                            if g == 0:
                                taken(pe, "ctxT")
                            pe.wait_ge(q["eps_q"], 2 * (g + 1))
                            k = begin(f"nd{g}")
                            for i in range(2):
                                for j in range(2):
                                    ins = pe.matmul(ps[M * j:M * (j + 1), k + i, 0:W2C],
                                                    ctx_d[:, g, M * j:M * (j + 1)],
                                                    fq[:, 2 * g + j, W2C * i:W2C * (i + 1)], start=True, stop=True)
                            end(ins, f"nd{g}")
                        for t in range(TT):
                            yield AT[f"ndT{t}"]
                            if t == 0:
                                taken(pe, f"nd{NG - 1}")
                            turn_nd(f"ndT{t}", t, nd)
                        yield AT["aT"]
                        taken_all(pe, [f"ndT{t}" for t in range(TT)])
                        turn("aT", at)
                        yield AT["aT4"]
                        turn("aT4", at)
                        yield AT["wo"]
                        taken_all(pe, ["aT", "aT4"])
                        project_rows("wo", wo_s, 0, aT)
                        yield AT["wo4"]
                        project_rows("wo4", wo_s, 0, aT)

                    item = 0

                    def first(i):
                        nonlocal item
                        h, t = GH * (i // 20) + i % GH, i % 20 // GH
                        for half in range(2):
                            bank_free(pe, a_before["s1", item])
                            n = W2C - half
                            pe.matmul(ps[0:TP, a_bank["s1", item], 0:n], sa[0:SK, h, cols(t)],
                                      sk[0:SK, h, W2C * half:W2C * half + n],
                                      start=True, stop=True).then_inc(q["s1_ready"], 1)
                            item += 1

                    def first_rows(g):
                        nonlocal item
                        assert item == rows_item(g)
                        bank_free(pe, a_before["s1", item])
                        pe.wait_ge(q["neg_parts"], g + 1)
                        for t in range(TT):
                            ins = pe.transpose(
                                ps[0:NPART * GH, a_bank["s1", item], :].bitcast(BF16)[:, 106 * t:106 * t + TP],
                                neg_p[:, g, t, :, :].rearrange("p k h -> p (k h)"), ident_b[0:TP, 0:TP])
                        ins.then_inc(q["s1_ready"], 1)
                        item += 1

                    def second(i):
                        h, t = GH * (i // 20) + i % GH, i % 20 // GH
                        if i % 20 == 0:
                            pe.wait_ge(q["neg_in"], 16 * NPART * (i // 20 + 1))
                        for half in range(2):
                            bank_free(pe, a_before["s2", 2 * i + half])
                            pe.matmul(ps[0:TP, a_bank["s2", 2 * i + half], 0:W2C], sk[:, h, cols(t)],
                                      sa[:, h, W2C * half:W2C * (half + 1)],
                                      start=True, stop=True).then_inc(q["s2_ready"], 1)

                    def weigh(n):
                        g, t = n // TT, n % TT
                        pe.wait_ge(q["s2_free"], 2 * GH * (n + 1))
                        if n == 0 and with_a:
                            taken(pe, GUESTS[-1])
                        if t == 0 and g:
                            pe.wait_ge(q["pv_free"], g)
                        for half in range(2):
                            for j in range(GH):
                                ins = pe.matmul(ps[32 * j:32 * (j + 1), PV_BANK + half, 0:W2C],
                                                va[:, t, GH * g + j, :],
                                                pT[:, n % 2, j, W2C * half:W2C * (half + 1)],
                                                start=(t == 0), stop=(t == TT - 1))
                        ins.then_inc(q["p_used"], 1)

                    def pass_b():
                        yield EARLY
                        pe.wait_ge(q["ym"], len(BANDS) + 1)
                        turn("yT", ym, 1)
                        yield EARLY + 1
                        turn("yT4", ym, 1)
                        taken_all(pe, ["yT", "yT4"])
                        pe.wait_ge(q["ones"], 1)
                        for i, pre in enumerate("QK"):
                            for g in range(2):
                                yield EARLY + 2 + 2 * i + g
                                project(f"{pre}{g}", w1_s, HID + C * i + CH * g, CH, yT, 1)
                        for i, name in enumerate(("V", "V4")):
                            yield EARLY + 6 + i
                            project_rows(name, w1_s, HID + 2 * C, yT, 1)
                        for step in range(NS + OFF + PV_LAG + 1):
                            yield PRE + step
                            if step == 0:
                                taken(pe, "g1")
                                pe.wait_ge(q["stack_b"], 16 * BLOCKS * 2)
                            if step == HIDDEN_END:
                                taken(pe, HIDDEN[-1])
                            if step < NS:
                                first(step)
                            if step in ROWS_AT:
                                first_rows(ROWS_AT.index(step))
                            i = step - OFF
                            if 0 <= i < NS:
                                second(i)
                            n = i - PV_LAG - GH + 1
                            if n >= 0 and n % GH == 0:
                                weigh(n // GH)
                        pe.wait_ge(q["pv_free"], NG)
                        pe.wait_ge(q["s1_free"], item)
                        pe.wait_ge(q["s2_free"], 2 * NS)
                        for t in range(TT):
                            yield ATT + t
                            turn_nd(f"NdT{t}", t, ndb)
                        taken_all(pe, [f"NdT{t}" for t in range(TT)])
                        yield ATT + TT
                        turn("AT", atb)
                        yield ATT + TT + 1
                        turn("AT4", atb)
                        taken_all(pe, ["AT", "AT4"])
                        for t in range(TT):
                            yield ATT + TT + 2 + t
                            k = begin(f"z{t}")
                            for f in range(HID // 128):
                                pe.matmul(ps[0:TP, k, 0:C], gT[:, f, cols(t)], w2h_s[:, f, :],
                                          start=(f == 0), stop=False)
                            for g in range(2):
                                ins = pe.matmul(ps[0:TP, k, 0:C], aTb[:, g, cols(t)], w2a_s[:, g, :],
                                                start=False, stop=(g == 1))
                            end(ins, f"z{t}")

                    def pass_h():
                        for f, name in enumerate(HIDDEN):
                            yield HIDDEN_AT[name]
                            project(name, w1_s, 128 * f, 128, yT, 1)

                    run(pass_a, pass_b, pass_h=pass_h)

                @block.scalar
                def _(act):
                    def out_of(name, dst, src, func=ACT.Copy, scale=1.0):
                        filled(act, name)
                        takes(act.activation(dst, src, func, scale=scale), name)

                    def turned(name, dst):
                        if name.endswith("4"):
                            out_of(name, dst[:, :, 4 * TP:K], ps[0:CH, bank(name):bank(name) + 2, 0:TP])
                        else:
                            out_of(name, dst[:, :, 0:4 * TP], ps[0:CH, bank(name):bank(name) + 2, 0:4 * TP])

                    def values(name, dst):
                        if name.endswith("4"):
                            out_of(name, dst[:, 4, :, 0:DH],
                                   ps[0:TP, bank(name), 0:C].rearrange("p (h d) -> p h d", h=H))
                            return
                        filled(act, name)
                        for i in range(2):
                            ins = act.activation(dst[:, 2 * i:2 * i + 2, :, 0:DH],
                                                 ps[0:TP, bank(name) + i, 0:2 * C].rearrange(
                                                     "p (t h d) -> p t h d", t=2, h=H), ACT.Copy)
                        takes(ins, name)

                    def pass_a():
                        for name in ("xT", "xT4"):
                            yield AT[name]
                            turned(name, xT)
                        for i, pre in enumerate("qk"):
                            for g in range(2):
                                yield AT[f"{pre}{g}"]
                                filled(act, f"{pre}{g}")
                                act.activation(split2(part[i][:, 0, g, :]), halves(f"{pre}{g}"), ACT.Copy)
                                act.activation(split2(sq[:, i, g, :]), halves(f"{pre}{g}"),
                                               ACT.Square).then_inc(q["sq"], 1)
                                taken(act, f"{pre}{g}")
                                act.activation(part[i][:, 1, g, :], left[i][:, g, :], ACT.Copy).then_inc(q["mid"], 1)
                        for name in ("v", "v4"):
                            yield AT[name]
                            values(name, vp)
                        yield AT["ss"] - 1
                        out_of("ssT", split2(ssT), halves("ssT", 64))
                        yield AT["ss"]
                        filled(act, "ss")
                        v = ps[0:TP, bank("ss"), 0:64 * TT].rearrange("p (t i h) -> p i t h", i=2, h=32)
                        for i in range(2):
                            ins = act.activation(squares[:, i, :, :], v[:, i, :, 0:H], ACT.Copy)
                        takes(ins, "ss")
                        yield AT["shift"]
                        out_of("shift", sh_row[:, 0:K].rearrange("p (t c) -> p t c", t=TT),
                               ps[0:2 * NPART * H, bank("shift"), :].bitcast(BF16)[:, 0:106 * TT].rearrange(
                                   "p (t c) -> p t c", t=TT)[:, :, 0:TP])
                        for t in range(TT):
                            yield AT[f"fk{t}"]
                            out_of(f"fk{t}", fk[:, t, :], wide(f"fk{t}"), ACT.Exp, DH ** -0.25)
                        for p in range(H // 2):
                            yield AT[f"fq{p}"]
                            out_of(f"fq{p}", split2(fq[:, p, :]), halves(f"fq{p}", 128), ACT.Exp, DH ** -0.25)
                        yield AT["ctx"]
                        out_of("ctx", cT[:, :, :].rearrange("p g (j m) -> p g j m", j=2),
                               ps[:, bank("ctx"), 0:NG * M].rearrange("p (g m) -> p g m", g=NG).unsqueeze(
                                   2).to_broadcast([128, NG, 2, M]))
                        for g in range(NG):
                            yield AT[f"nd{g}"]
                            out_of(f"nd{g}", split2(nd[:, g, :]), halves(f"nd{g}", 128))
                        for name in ("aT", "aT4"):
                            yield AT[name]
                            turned(name, aT)
                        yield AT["prob"]
                        act.wait_ge(q["logits"], 1)
                        act.activation(pr[:, 0, :, :], pr[:, 1, :, :], ACT.Exp).then_inc(q["exps"], 1)

                    def gathered(g):
                        act.wait_ge(q["p_used"], TT * (g + 1))
                        act.activation(split2(ndb[:, g, :]), ps[:, PV_BANK:PV_BANK + 2, 0:W2C],
                                       ACT.Copy).then_inc(q["pv_free"], 1)

                    def pass_b():
                        for i, (name, c) in enumerate((("yT", slice(0, 4 * TP)), ("yT4", slice(4 * TP, K)))):
                            yield EARLY + i
                            filled(act, name)
                            n = c.stop - c.start
                            act.activation(yT[0:CH, 0, c], ps[0:CH, bank(name), 0:n], ACT.Copy)
                            takes(act.activation(yT[:, 1, c], ps[0:CH + 1, bank(name) + 1, 0:n], ACT.Copy), name)
                        for i, pre in enumerate("QK"):
                            for g in range(2):
                                yield EARLY + 2 + 2 * i + g
                                filled(act, f"{pre}{g}")
                                act.activation(split2(part_b[i][:, 0, g, :]), halves(f"{pre}{g}"),
                                               ACT.Copy).then_inc(q["hi_b"], 1)
                                taken(act, f"{pre}{g}")
                                act.activation(part_b[i][:, 1, g, :], left_b[:, g, :], ACT.Copy).then_inc(q["mid_b"], 1)
                        for i, name in enumerate(("V", "V4")):
                            yield EARLY + 6 + i
                            values(name, va)
                        for i in range(NS):
                            yield PRE + OFF + i
                            n = i // GH
                            for half in range(2):
                                act.wait_ge(q["s2_ready"], 2 * i + half + 1)
                                if n >= 2 and half == 0:
                                    act.wait_ge(q["p_used"], n - 1)
                                act.activation(pT[:, n % 2, i % GH, W2C * half:W2C * (half + 1)],
                                               ps[0:TP, a_bank["s2", 2 * i + half], 0:W2C],
                                               ACT.Exp, scale=DH ** -0.5).then_inc(q["s2_free"], 1)
                            if i >= 20 and i % 20 == 3:
                                gathered(i // 20 - 1)
                        yield ATT
                        gathered(NG - 1)
                        for i, name in enumerate(("AT", "AT4")):
                            yield ATT + TT + i
                            turned(name, aTb)

                    def pass_h():
                        for f, name in enumerate(HIDDEN):
                            yield HIDDEN_AT[name]
                            if f == 0:
                                for sem_ in away_sem[2]:
                                    act.wait_ge(sem_, 16)
                                act.wait_ge(q["lo_b"], 4)
                            out_of(name, split2(gT[:, f, :]), halves(name, 128), ACT.Gelu)

                    run(pass_a, pass_b, pass_h=pass_h)

                @block.gpsimd
                def _(pool):
                    def inverse_root(i):
                        pool.wait_ge(q[f"var{i + 1}"], 1)
                        pool.tensor_tensor(rstd[:, i, :], var_e[:, i, :], neg_half[:, :],
                                           ALU.pow).then_inc(q[f"rstd{i + 1}"], 1)

                    def pass_a():
                        for i, pre in enumerate("qk"):
                            for g in range(2):
                                yield AT[f"{pre}{g}"]
                                pool.wait_ge(q["mid"], 2 * i + g + 1)
                                pool.tensor_tensor(part[i][:, 2, g, :], left[i][:, g, :], part[i][:, 1, g, :],
                                                   ALU.subtract).then_inc(q["lo"], 1)
                        yield AT["top"]
                        pool.wait_ge(q["top"], 1)
                        pool.partition_all_reduce(top_k[:, 1, :], top_k[:, 0, :], TP, RMAX).then_inc(q["top_all"], 1)
                        for t in range(TT):
                            yield AT[f"fk{t}"]
                            taken(pool, f"fk{t}")
                            pool.tensor_scalar(fk[:, t, :], fk[:, t, :], 1e-4, None, ALU.add).then_inc(q["eps_k"], 1)
                        for p in range(H // 2):
                            yield AT[f"fq{p}"]
                            taken(pool, f"fq{p}")
                            pool.tensor_scalar(fq[:, p, :], fq[:, p, :], 1e-4, None, ALU.add).then_inc(q["eps_q"], 1)
                        yield AT["wo4"]
                        inverse_root(1)
                        inverse_root(2)
                        yield AT["prob"]
                        pool.wait_ge(q["y"], TT)
                        pool.tensor_tensor(y[:, :, :], y[:, :, :],
                                           gamma_s[:, :].unsqueeze(1).to_broadcast([TP, TT, C]),
                                           ALU.mult).then_inc(q["gamma"], 1)
                        pool.wait_ge(q["gamma"], 1)
                        pool.tensor_tensor(y[:, :, :], y[:, :, :],
                                           beta_s[:, :].unsqueeze(1).to_broadcast([TP, TT, C]),
                                           ALU.add).then_inc(q["beta"], 1)

                    def pass_b():
                        yield 0
                        pool.tensor_tensor(base_b[:, :, :], h1[:, :, :], u[:, :, :], ALU.add).then_inc(q["kept"], 1)
                        for i in range(2):
                            for g in range(2):
                                yield EARLY + 2 + 2 * i + g
                                pool.wait_ge(q["mid_b"], 2 * i + g + 1)
                                pool.tensor_tensor(part_b[i][:, 2, g, :], left_b[:, g, :], part_b[i][:, 1, g, :],
                                                   ALU.subtract).then_inc(q["lo_b"], 1)

                    def pass_c():
                        yield AT["ln1"]
                        if not with_a:
                            pool.memset(vp[:, :, :, DH:], 1.0).then_inc(q["constant_p"], 1)
                            pool.memset(va[:, :, :, DH:], 1.0).then_inc(q["constant_p"], 1)
                            pool.memset(sh_row[:, :], 0.0).then_inc(q["constant_p"], 1)
                            pool.memset(rows[:, :, :], 0.0).then_inc(q["constant_p"], 1)
                            pool.wait_ge(q["constant_p"], 4)
                        inverse_root(0)

                    run(pass_a, pass_b, pass_c)

                @block.vector
                def _(dve):
                    n = 0

                    def go(ins):
                        nonlocal n
                        n += 1
                        ins.then_inc(q["chain"], 1)

                    def settle():
                        dve.wait_ge(q["chain"], n)

                    def link(ins):
                        go(ins)
                        settle()

                    unread_by = []

                    def place():
                        if len(unread_by) >= UNREAD:
                            dve.wait_ge(q["chain"], unread_by[-UNREAD])
                        unread_by.append(n + 1)
                        return unread[:, len(unread_by) % UNREAD, :]

                    def statistics(src, i, eps, signal, slot, gap):
                        for t in range(TT):
                            yield slot + gap * t
                            go(dve.bn_stats(st[:, i, t, :], src[:, t, :]))
                        yield slot + gap * TT
                        settle()
                        for t in range(TT):
                            go(dve.bn_aggr(mv[:, i, t, :], st[:, i, t, :]))
                        settle()
                        dve.tensor_scalar(var_e[:, i, :], mv[:, i, :, 1], eps, None, ALU.add).then_inc(q[signal], 1)

                    def normalized(dst, src, i, signal, slot, gap):
                        for t in range(TT):
                            yield slot + gap * t
                            if t == 0:
                                dve.wait_ge(q[f"rstd{i + 1}"], 1)
                            dve.tensor_scalar(dst[:, t, :], src[:, t, :], mv[:, i, t, 0:1], rstd[:, i, t:t + 1],
                                              ALU.subtract, ALU.mult).then_inc(q[signal], 1)

                    def divided(name, i, t, dst):
                        filled(dve, name)
                        v = ps[0:TP, bank(name), 0:NG * 128].rearrange("p (h c) -> p h c", c=2 * DH)
                        link(dve.reciprocal(den[:, i, t, :], v[:, :, DH]))
                        takes(dve.tensor_tensor(dst[:, t, :].rearrange("p (h d) -> p h d", d=DH), v[:, :, 0:DH],
                                                den[:, i, t, :].unsqueeze(2).to_broadcast([TP, H, DH]), ALU.mult),
                              name)

                    def pass_a():
                        for i, pre in enumerate("qk"):
                            for g in range(2):
                                name = f"{pre}{g}"
                                yield AT[name] + LEFT_AT
                                dve.wait_ge(q["sq"], 2 * i + g + 1)
                                takes(dve.tensor_tensor(split2(left[i][:, g, :]), halves(name),
                                                        split2(part[i][:, 0, g, :]), ALU.subtract), name)
                        for i, pre in enumerate(("mq", "mk")):
                            for t in range(TT):
                                yield AT[f"{pre}{t}"]
                                filled(dve, f"{pre}{t}")
                                takes(dve.tensor_reduce(top[:, i, t, :],
                                                        wide(f"{pre}{t}").rearrange("p (h m) -> p h m", m=M), AX.X,
                                                        ALU.max), f"{pre}{t}")
                        yield AT["top"]
                        taken(dve, f"mk{TT - 1}")
                        dve.tensor_reduce(top_k[:, 0, :], top[:, 1, :, :].rearrange("p t h -> p h t"), AX.X,
                                          ALU.max).then_inc(q["top"], 1)
                        go(dve.scalar_tensor_tensor(out=shift[:, 0, :, :], in0=squares[:, 0, :, :], scalar=-0.25,
                                                    in1=top[:, 0, :, :], op0=ALU.mult, op1=ALU.subtract))
                        yield AT["shift"]
                        dve.wait_ge(q["top_all"], 1)
                        link(dve.scalar_tensor_tensor(
                            out=shift[:, 1, :, :], in0=squares[:, 1, :, :], scalar=-0.25,
                            in1=top_k[:, 1, :].unsqueeze(1).to_broadcast([TP, TT, H]),
                            op0=ALU.mult, op1=ALU.subtract))
                        p = [sh_p[:, :, :, k, :].rearrange("p t i h -> p i t h") for k in range(NPART)]
                        for i in range(2):
                            go(dve.tensor_copy(p[0][:, i], shift[:, i, :, :]))
                        settle()
                        link(dve.tensor_tensor(sh_l[:, :, :, :], shift[:, :, :, :], p[0], ALU.subtract))
                        link(dve.tensor_copy(p[1], sh_l[:, :, :, :]))
                        dve.tensor_tensor(p[2], sh_l[:, :, :, :], p[1], ALU.subtract).then_inc(q["shift_parts"], 1)
                        yield AT["ctxT"]
                        filled(dve, "ctxT")
                        src = ps[:, bank("ctxT"), 0:NG * 128].rearrange("p (g j c) -> p g j c", j=2, c=2 * DH)
                        dst = ctx_d[:, :, :].rearrange("p g c -> p (g c)").rearrange("p (g j c) -> p g j c", j=2,
                                                                                     c=2 * DH)
                        dve.tensor_copy(dst[0:M, :, 0, :], src[0:M, :, 0, :])
                        takes(dve.tensor_copy(dst[M:, :, 1, :], src[M:, :, 1, :]), "ctxT")
                        for t in range(TT):
                            yield AT[f"ndT{t}"]
                            divided(f"ndT{t}", 0, t, at)
                        for t in range(TT):
                            name = "wo" if t < TT - 1 else "wo4"
                            if t in (0, TT - 1):
                                yield AT[name]
                            if t == 0:
                                dve.wait_ge(q["h_in"], 16)
                            filled(dve, name)
                            ins = dve.tensor_tensor(h1[:, t, :], tok[:, t, :], tile_of("wo", "wo4", t), ALU.add)
                            if t >= TT - 2:
                                takes(ins, name)
                        yield AT["ln2"]
                        taken_all(dve, ["wo", "wo4"])
                        yield from statistics(h1, 1, 1e-5, "var2", AT["ln2"], SPREAD["norm"])
                        yield from normalized(u, h1, 1, "u", AT["u"], SPREAD["norm"])
                        yield AT["ln3"]
                        dve.wait_ge(q["u"], TT)
                        yield from statistics(u, 2, 1e-6, "var3", AT["ln3"], SPREAD["norm"])
                        for t in range(TT):
                            for e in range(E):
                                yield AT["router"] + SPREAD["router"] * (t + e / E)
                                go(dve.tensor_tensor_reduce(place()[:, 0:C], u[:, t, :], wr_s[:, e, :], 1.0, 0.0,
                                                            ALU.mult, ALU.add, lg[:, t, e:e + 1]))
                        yield AT["prob"]
                        settle()
                        link(dve.tensor_reduce(lg_s[:, 0, :], lg[:, :, :], AX.X, ALU.max))
                        dve.tensor_tensor(pr[:, 1, :, :], lg[:, :, :],
                                          lg_s[:, 0, :].unsqueeze(2).to_broadcast([TP, TT, E]),
                                          ALU.subtract).then_inc(q["logits"], 1)
                        yield AT["y"]
                        if with_b:
                            filled(dve, "yT4")
                        yield from normalized(y, u, 2, "y", AT["y"], SPREAD["norm"])
                        yield AT["exps"]
                        dve.wait_ge(q["exps"], 1)
                        link(dve.tensor_reduce(lg_s[:, 1, :], pr[:, 0, :, :], AX.X, ALU.add))
                        link(dve.reciprocal(lg_s[:, 2, :], lg_s[:, 1, :]))
                        dve.tensor_tensor(pr[:, 2, :, :], pr[:, 0, :, :],
                                          lg_s[:, 2, :].unsqueeze(2).to_broadcast([TP, TT, E]),
                                          ALU.mult).then_inc(q["prob"], 1)

                    item = 0

                    def maxima(g):
                        dve.wait_ge(q["s1_free"], item)
                        r0, r1 = neg[:, 0, :, :], neg[:, 1, :, :]
                        p = [neg_p[:, g, :, k, :] for k in range(NPART)]
                        link(dve.tensor_reduce(r0, mxh[:, GH * g:GH * (g + 1), :, :].rearrange("p h t a -> p t h a"),
                                               AX.X, ALU.max, negate=True))
                        link(dve.tensor_copy(p[0], r0))
                        link(dve.tensor_tensor(r1, r0, p[0], ALU.subtract))
                        link(dve.tensor_copy(p[1], r1))
                        dve.tensor_tensor(p[2], r1, p[1], ALU.subtract).then_inc(q["neg_parts"], 1)
                        dve.wait_ge(q["neg_parts"], g + 1)

                    def pass_b():
                        nonlocal item
                        yield 0
                        dve.memset(yT[:, :, K:], 0.0).then_inc(q["ones"], 1)
                        for t in range(TT):
                            for e in range(E):
                                yield RANKS_AT + SPREAD["ranks"] * (t + e / E)
                                go(dve.scalar_tensor_tensor(out=place().bitcast(BF16)[:, 0:K], in0=prow[:, :, e],
                                                            scalar=pr[:, 2, t, e:e + 1], in1=tie[:, t, :],
                                                            op0=ALU.subtract, op1=ALU.is_gt,
                                                            accum_out=rank2[:, t, e:e + 1]))
                        settle()
                        link(dve.tensor_scalar(chosen[:, :, :], rank2[:, :, :].rearrange("p t e -> p e t"),
                                               float(CAP), None, ALU.is_lt))
                        link(dve.tensor_tensor(gate[:, :, :], chosen[:, :, :],
                                               pr[:, 2, :, :].rearrange("p t e -> p e t"), ALU.mult))
                        for e in range(E - 2, -1, -1):
                            go(dve.tensor_tensor(chosen[:, e, :], chosen[:, e, :], chosen[:, e + 1, :], ALU.add))
                            link(dve.tensor_tensor(gate[:, e, :], gate[:, e, :], gate[:, e + 1, :], ALU.add))
                        for e, (lo, hi) in enumerate(BANDS):
                            dve.tensor_tensor(y[:, :, lo:hi], y[:, :, lo:hi],
                                              chosen[:, e, :].unsqueeze(2).to_broadcast([TP, TT, hi - lo]),
                                              ALU.mult).then_inc(q["ym"], 1)
                        dve.tensor_copy(ym[:, :, C:], chosen[:, 0, :].unsqueeze(2)).then_inc(q["ym"], 1)
                        for i, pre in enumerate("QK"):
                            for g in range(2):
                                name = f"{pre}{g}"
                                yield EARLY + 2 + 2 * i + g
                                dve.wait_ge(q["hi_b"], 2 * i + g + 1)
                                if i:
                                    dve.wait_ge(q["lo_b"], g + 1)
                                takes(dve.tensor_tensor(split2(left_b[:, g, :]), halves(name),
                                                        split2(part_b[i][:, 0, g, :]), ALU.subtract), name)
                        for step in range(ROWS_AT[-1] + 1):
                            yield PRE + step
                            if step < NS:
                                h, t = GH * (step // 20) + step % GH, step % 20 // GH
                                for half in range(2):
                                    dve.wait_ge(q["s1_ready"], item + 1)
                                    dve.tensor_reduce(mxh[:, h, t, half:half + 1],
                                                      ps[0:TP, a_bank["s1", item], 0:W2C - half],
                                                      AX.X, ALU.max).then_inc(q["s1_free"], 1)
                                    item += 1
                            if step % 20 == 19 and step < NS:
                                maxima(step // 20)
                            if step in ROWS_AT:
                                g = ROWS_AT.index(step)
                                dve.wait_ge(q["s1_ready"], item + 1)
                                dve.tensor_copy(
                                    rows[:, g, 0:K].rearrange("p (t c) -> p t c", t=TT),
                                    ps[0:NPART * GH, a_bank["s1", item], :].bitcast(BF16)[:, 0:106 * TT].rearrange(
                                        "p (t c) -> p t c", t=TT)[:, :, 0:TP]).then_inc(q["s1_free"], 1)
                                item += 1
                        for t in range(TT):
                            yield ATT + t
                            divided(f"NdT{t}", 1, t, atb)
                        dve.wait_ge(q["kept"], 1)
                        for t in range(TT):
                            yield ATT + TT + 2 + t
                            filled(dve, f"z{t}")
                            takes(dve.tensor_tensor(z[:, t, :], ps[0:TP, bank(f"z{t}"), 0:C], b2_s[:, :], ALU.add),
                                  f"z{t}")
                            taken(dve, f"z{t}")
                            for e, (lo, hi) in enumerate(BANDS):
                                dve.scalar_tensor_tensor(out=z[:, t, lo:hi], in0=z[:, t, lo:hi],
                                                         scalar=gate[:, e, t:t + 1], in1=base_b[:, t, lo:hi],
                                                         op0=ALU.mult, op1=ALU.add).then_inc(q["res"], 1)

                    def pass_c():
                        yield AT["ln1"]
                        if not with_a:
                            dve.memset(sk[ONES_FROM:, :, :], 1.0).then_inc(q["constant_v"], 1)
                            dve.memset(xT[:, :, K:], 0.0).then_inc(q["constant_v"], 1)
                            dve.memset(ctx_d[:, :, :], 0.0).then_inc(q["constant_v"], 1)
                            dve.wait_ge(q["constant_v"], 3)
                        dve.wait_ge(q["tok_in"], 16)
                        yield from statistics(xn, 0, 1e-5, "var1", AT["ln1"], SPREAD["norm"])
                        yield from normalized(xn, xn, 0, "xn", AT["xn"], SPREAD["norm"])

                    run(pass_a, pass_b, pass_c)
            nc.all_engine_barrier(sems_to_clear=every)

        one_round(0, None, None)
        one_round(1, 0, None)
        one_round(2, 1, 0)
        with nc.Fori(2, B - 1) as b:
            one_round(b + 1, b, b - 1, b - 2)
        one_round(None, B - 1, B - 2, B - 3)
        one_round(None, None, B - 1, B - 2, last=True)


def kernel(x, L0_tok_w, L0_tok_b, L0_attn_Wq, L0_attn_Wk, L0_attn_Wv, L0_attn_Wo, L0_attn_proj, L0_ffn_w_router,
           L0_ffn_gamma1, L0_ffn_beta1, L0_ffn_w1, L0_ffn_b1, L0_ffn_w2, L0_ffn_b2):
    import numpy as np
    import concourse.bacc as bacc
    from concourse.bass_utils import run_bass_kernel_spmd

    nc = bacc.Bacc("TRN2", target_bir_lowering=False, num_devices=1)
    laid = {
        "x": x, "tok_w": np.asarray(L0_tok_w).reshape(1, C), "tok_b": np.asarray(L0_tok_b).reshape(1, 1),
        "wq": L0_attn_Wq, "wk": L0_attn_Wk, "wv": L0_attn_Wv, "wo": L0_attn_Wo,
        "projT": np.asarray(L0_attn_proj).T, "wr": L0_ffn_w_router,
        "gamma": np.asarray(L0_ffn_gamma1).reshape(1, C), "beta": np.asarray(L0_ffn_beta1).reshape(1, C),
        "w1T": np.asarray(L0_ffn_w1).T, "b1": np.asarray(L0_ffn_b1).reshape(1, FC1),
        "w2T": np.asarray(L0_ffn_w2).T, "b2": np.asarray(L0_ffn_b2).reshape(1, 2 * C),
    }
    arrays = {f"in_{name}": np.ascontiguousarray(a) for name, a in laid.items()}
    aps = [nc.dram_tensor(name, a.shape, mybir.dt.from_np(a.dtype), kind="ExternalInput").ap()
           for name, a in arrays.items()]
    out = nc.dram_tensor("out_0", (B, K, C), F32, kind="ExternalOutput").ap()
    tower(nc, *aps, out)
    r = run_bass_kernel_spmd(nc, [arrays], core_ids=[0])
    return r.results[0]["out_0"]
```
